# Optimizing a Trainium2 kernel written in Bass

```python
import numpy as np
import jax
import jax.numpy as jnp

def _softmax(x, axis=-1):
    return jax.nn.softmax(x, axis=axis)

def _gelu(x):
    return jax.nn.gelu(x, approximate=True)

def _silu(x):
    return jax.nn.silu(x)

def _sigmoid(x):
    return jax.nn.sigmoid(x)

def _layernorm(x, axis=-1, eps=1e-05):
    m = jnp.mean(x, axis=axis, keepdims=True)
    v = jnp.var(x, axis=axis, keepdims=True)
    return (x - m) / jnp.sqrt(v + eps)

def _scatter_add(tgt, idx, src, axis=0):
    return tgt.at[idx].add(src)

def _segment_sum(src, seg, n):
    return jax.ops.segment_sum(src, seg, n)
kernel_name = 'mk_gnn_resnorm_d4_gnn_r32_e31836'

def setup_inputs(seed: int=0):
    np.random.seed(seed)
    _w = jnp.asarray

    def _rec_inputs():
        import jax
        import jax.numpy as jnp
        _gk = jax.random.key(seed)
        x = -0.0002117 + 1 * jax.random.normal(jax.random.fold_in(_gk, 1), (3125, 256), jnp.float32)
        _s = jax.random.randint(jax.random.fold_in(_gk, 2), (25000,), 0, 3125, jnp.int32)
        _d = jax.random.randint(jax.random.fold_in(_gk, 3), (25000,), 0, 3125, jnp.int32)
        _loop = jnp.arange(3125, dtype=jnp.int32)
        src = jnp.concatenate([_s, _d, _loop])
        dst = jnp.concatenate([_d, _s, _loop])
        _o = jnp.argsort(dst, stable=True)
        src = src[_o]
        dst = dst[_o]
        edge_type_500 = jax.random.randint(jax.random.fold_in(_gk, 12), (53125,), 0, 500, jnp.int32)
        return (x, src, dst, edge_type_500)
    x, src, dst, edge_type_500 = _rec_inputs()

    def _L0_gnn_setup():
        import jax, jax.numpy as jnp
        import numpy as np
        N_NODES = 3125
        N_EDGES = 100000
        D_IN = 256
        D_OUT = 256
        LEAKY_SLOPE = 0.01
        key = jax.random.key(seed)
        ks = jax.random.split(key, 8)
        s_in = 1.0 / np.sqrt(D_IN)
        s_out = 1.0 / np.sqrt(D_OUT)
        return {'features': jax.random.normal(ks[0], (N_NODES, D_IN), dtype=jnp.float32), 'indices': jax.random.randint(ks[1], (2, N_EDGES), 0, N_NODES, dtype=jnp.int64), 'W_layer': jax.random.uniform(ks[2], (D_OUT, D_IN), jnp.float32, -s_in, s_in), 'b_layer': jax.random.uniform(ks[3], (D_OUT,), jnp.float32, -s_in, s_in), 'w_a1': jax.random.uniform(ks[4], (1, D_OUT), jnp.float32, -s_out, s_out), 'b_a1': jax.random.uniform(ks[5], (1,), jnp.float32, -s_out, s_out), 'w_a2': jax.random.uniform(ks[6], (1, D_OUT), jnp.float32, -s_out, s_out), 'b_a2': jax.random.uniform(ks[7], (1,), jnp.float32, -s_out, s_out)}
    _L0_gnn_all = _L0_gnn_setup()
    _L0_gnn_in = {k: v for k, v in _L0_gnn_all.items() if k in ('W_layer', 'b_layer', 'w_a1', 'b_a1', 'w_a2', 'b_a2')}
    del _L0_gnn_all

    def _L1_gnn_setup():
        import jax, jax.numpy as jnp
        import numpy as np
        N_NODES = 50000
        N_EDGES = 25000
        D = 256
        LN_EPS = 1e-05

        def _layer_norm(h, gamma, beta):
            mu = jnp.mean(h, axis=-1, keepdims=True)
            var = jnp.mean((h - mu) ** 2, axis=-1, keepdims=True)
            return (h - mu) * jax.lax.rsqrt(var + LN_EPS) * gamma + beta
        key = jax.random.key(seed)
        ks = jax.random.split(key, 8)
        s = 1.0 / np.sqrt(D)
        x = jax.random.normal(ks[0], (N_NODES, D), dtype=jnp.float32)
        edge_index = jax.random.randint(ks[1], (2, N_EDGES), 0, N_NODES, dtype=jnp.int64)
        W_in = jax.random.normal(ks[2], (D, D), dtype=jnp.float32) * s
        b_in = jnp.zeros((D,), jnp.float32)
        Ws = jax.random.normal(ks[3], (3, D, D), dtype=jnp.float32) * s
        bs = jnp.zeros((3, D), jnp.float32)
        gamma = jnp.ones((D,), jnp.float32)
        beta = jnp.zeros((D,), jnp.float32)
        W_out = jax.random.normal(ks[4], (D, D), dtype=jnp.float32) * s
        b_out = jnp.zeros((D,), jnp.float32)
        return {'x': x, 'edge_index': edge_index, 'W_in': W_in, 'b_in': b_in, 'Ws': Ws, 'bs': bs, 'gamma': gamma, 'beta': beta, 'W_out': W_out, 'b_out': b_out}
    _L1_gnn_all = _L1_gnn_setup()
    _L1_gnn_in = {k: v for k, v in _L1_gnn_all.items() if k in ('W_in', 'b_in', 'Ws', 'bs', 'gamma', 'beta', 'W_out', 'b_out')}
    del _L1_gnn_all

    def _L2_gnn_setup():
        import jax, jax.numpy as jnp
        import numpy as np
        N, E, H, C, IN = (50000, 15625, 4, 64, 256)

        def _gat_conv(x, src, dst, W, a_src, a_dst, b, n_nodes):
            Hh, Cc = a_src.shape
            h = (x @ W).reshape(n_nodes, Hh, Cc)
            e_src = jnp.einsum('nhc,hc->nh', h, a_src)
            e_dst = jnp.einsum('nhc,hc->nh', h, a_dst)
            e = jax.nn.leaky_relu(e_src[src] + e_dst[dst], 0.2)
            m = jax.lax.stop_gradient(jax.ops.segment_max(e, dst, num_segments=n_nodes))
            ex = jnp.exp(e - m[dst])
            denom = jax.ops.segment_sum(ex, dst, num_segments=n_nodes)
            alpha = ex / (denom[dst] + 1e-16)
            out = jax.ops.segment_sum(h[src] * alpha[:, :, None], dst, num_segments=n_nodes)
            return out.reshape(n_nodes, Hh * Cc) + b
        key = jax.random.key(seed)
        ks = jax.random.split(key, 16)
        sW = 1.0 / np.sqrt(IN)
        sA = 1.0 / np.sqrt(C)
        inp = {'x': jax.random.normal(ks[0], (N, IN), jnp.float32), 'edge_index': jax.random.randint(ks[1], (2, E), 0, N, jnp.int64 if jax.config.jax_enable_x64 else jnp.int32), 'W1': jax.random.normal(ks[2], (IN, H * C), jnp.float32) * sW, 'as1': jax.random.normal(ks[3], (H, C), jnp.float32) * sA, 'ad1': jax.random.normal(ks[4], (H, C), jnp.float32) * sA, 'b1': jnp.zeros((H * C,), jnp.float32), 'W2': jax.random.normal(ks[5], (H * C, H * C), jnp.float32) * sW, 'as2': jax.random.normal(ks[6], (H, C), jnp.float32) * sA, 'ad2': jax.random.normal(ks[7], (H, C), jnp.float32) * sA, 'b2': jnp.zeros((H * C,), jnp.float32), 'WN': jax.random.normal(ks[8], (H * C, H * C), jnp.float32) * sW, 'asN': jax.random.normal(ks[9], (H, C), jnp.float32) * sA, 'adN': jax.random.normal(ks[10], (H, C), jnp.float32) * sA, 'bN': jnp.zeros((H * C,), jnp.float32)}
        return inp
    _L2_gnn_all = _L2_gnn_setup()
    _L2_gnn_in = {k: v for k, v in _L2_gnn_all.items() if k in ('W1', 'as1', 'ad1', 'b1', 'W2', 'as2', 'ad2', 'b2', 'WN', 'asN', 'adN', 'bN')}
    del _L2_gnn_all

    def _L3_gnn_setup():
        import jax, jax.numpy as jnp
        import numpy as np
        G = (1.0, 1.0)

        def to_hypercomplex(x, n_blades):
            return x.reshape(*x.shape[:-1], n_blades, -1).swapaxes(-2, -1)

        def clifford_kernel_2d(w, g):
            g0, g1 = g
            k0 = jnp.concatenate([w[0], g0 * w[1], g1 * w[2], -g0 * g1 * w[3]], axis=1)
            k1 = jnp.concatenate([w[1], w[0], -g1 * w[3], g1 * w[2]], axis=1)
            k2 = jnp.concatenate([w[2], g0 * w[3], w[0], -g0 * w[1]], axis=1)
            k3 = jnp.concatenate([w[3], w[2], w[1], w[0]], axis=1)
            return jnp.concatenate([k0, k1, k2, k3], axis=0)

        def clifford_linear(x, w, b, g=G):
            N = x.shape[0]
            k = clifford_kernel_2d(w, g)
            xf = x.swapaxes(-2, -1).reshape(N, -1)
            out = xf @ k.T + b.reshape(-1)
            C_out = w.shape[1]
            return out.reshape(N, 4, C_out).swapaxes(-2, -1)
        key = jax.random.key(seed)
        ks = jax.random.split(key, 10)
        N, E, R, emb_dim = (3125, 18750, 500, 256)
        C = emb_dim // 4
        s = 0.05
        return {'h': jax.random.normal(ks[0], (N, emb_dim), jnp.float32), 'edge_index': jax.random.randint(ks[1], (2, E), 0, N, jnp.int64), 'edge_type': jax.random.randint(ks[2], (E,), 0, R, jnp.int64), 'relation_emb': jax.random.normal(ks[3], (R, emb_dim), jnp.float32), 'msg_w': jax.random.normal(ks[4], (4, C, C), jnp.float32) * s, 'msg_b': jax.random.normal(ks[5], (4, C), jnp.float32) * s, 'upd_w': jax.random.normal(ks[6], (4, C, C), jnp.float32) * s, 'upd_b': jax.random.normal(ks[7], (4, C), jnp.float32) * s, 'gate_w': jax.random.normal(ks[8], (1, emb_dim), jnp.float32) * s, 'gate_b': jax.random.normal(ks[9], (1,), jnp.float32) * s}
    _L3_gnn_all = _L3_gnn_setup()
    _L3_gnn_in = {k: v for k, v in _L3_gnn_all.items() if k in ('relation_emb', 'msg_w', 'msg_b', 'upd_w', 'upd_b', 'gate_w', 'gate_b')}
    del _L3_gnn_all
    return {'x': x, 'src': src, 'dst': dst, 'edge_type_500': edge_type_500, 'L0_gnn_W_layer': _L0_gnn_in['W_layer'], 'L0_gnn_b_layer': _L0_gnn_in['b_layer'], 'L0_gnn_w_a1': _L0_gnn_in['w_a1'], 'L0_gnn_b_a1': _L0_gnn_in['b_a1'], 'L0_gnn_w_a2': _L0_gnn_in['w_a2'], 'L0_gnn_b_a2': _L0_gnn_in['b_a2'], 'L1_gnn_W_in': _L1_gnn_in['W_in'], 'L1_gnn_b_in': _L1_gnn_in['b_in'], 'L1_gnn_Ws': _L1_gnn_in['Ws'], 'L1_gnn_bs': _L1_gnn_in['bs'], 'L1_gnn_gamma': _L1_gnn_in['gamma'], 'L1_gnn_beta': _L1_gnn_in['beta'], 'L1_gnn_W_out': _L1_gnn_in['W_out'], 'L1_gnn_b_out': _L1_gnn_in['b_out'], 'L2_gnn_W1': _L2_gnn_in['W1'], 'L2_gnn_as1': _L2_gnn_in['as1'], 'L2_gnn_ad1': _L2_gnn_in['ad1'], 'L2_gnn_b1': _L2_gnn_in['b1'], 'L2_gnn_W2': _L2_gnn_in['W2'], 'L2_gnn_as2': _L2_gnn_in['as2'], 'L2_gnn_ad2': _L2_gnn_in['ad2'], 'L2_gnn_b2': _L2_gnn_in['b2'], 'L2_gnn_WN': _L2_gnn_in['WN'], 'L2_gnn_asN': _L2_gnn_in['asN'], 'L2_gnn_adN': _L2_gnn_in['adN'], 'L2_gnn_bN': _L2_gnn_in['bN'], 'L3_gnn_relation_emb': _L3_gnn_in['relation_emb'], 'L3_gnn_msg_w': _L3_gnn_in['msg_w'], 'L3_gnn_msg_b': _L3_gnn_in['msg_b'], 'L3_gnn_upd_w': _L3_gnn_in['upd_w'], 'L3_gnn_upd_b': _L3_gnn_in['upd_b'], 'L3_gnn_gate_w': _L3_gnn_in['gate_w'], 'L3_gnn_gate_b': _L3_gnn_in['gate_b']}

def reference(x, src, dst, edge_type_500, L0_gnn_W_layer, L0_gnn_b_layer, L0_gnn_w_a1, L0_gnn_b_a1, L0_gnn_w_a2, L0_gnn_b_a2, L1_gnn_W_in, L1_gnn_b_in, L1_gnn_Ws, L1_gnn_bs, L1_gnn_gamma, L1_gnn_beta, L1_gnn_W_out, L1_gnn_b_out, L2_gnn_W1, L2_gnn_as1, L2_gnn_ad1, L2_gnn_b1, L2_gnn_W2, L2_gnn_as2, L2_gnn_ad2, L2_gnn_b2, L2_gnn_WN, L2_gnn_asN, L2_gnn_adN, L2_gnn_bN, L3_gnn_relation_emb, L3_gnn_msg_w, L3_gnn_msg_b, L3_gnn_upd_w, L3_gnn_upd_b, L3_gnn_gate_w, L3_gnn_gate_b):
    import jax
    import jax.numpy as jnp

    def _L0_gnn_ref(features, indices, W_layer, b_layer, w_a1, b_a1, w_a2, b_a2):
        import jax, jax.numpy as jnp
        import numpy as np
        N_NODES = 3125
        N_EDGES = 100000
        D_IN = 256
        D_OUT = 256
        LEAKY_SLOPE = 0.01
        n = features.shape[0]
        h = features @ W_layer.T + b_layer
        a1 = (h @ w_a1.T + b_a1)[:, 0]
        a2 = (h @ w_a2.T + b_a2)[:, 0]
        row = indices[0]
        col = indices[1]
        v = jax.nn.leaky_relu(a1[row] + a2[col], negative_slope=LEAKY_SLOPE)
        m = jax.ops.segment_max(v, row, num_segments=n)
        ev = jnp.exp(v - m[row])
        s = jax.ops.segment_sum(ev, row, num_segments=n)
        att = ev / s[row]
        out = jax.ops.segment_sum(att[:, None] * h[col], row, num_segments=n)
        return out

    def _L1_gnn_ref(x, edge_index, W_in, b_in, Ws, bs, gamma, beta, W_out, b_out):
        import jax, jax.numpy as jnp
        import numpy as np
        N_NODES = 50000
        N_EDGES = 25000
        D = 256
        LN_EPS = 1e-05

        def _layer_norm(h, gamma, beta):
            mu = jnp.mean(h, axis=-1, keepdims=True)
            var = jnp.mean((h - mu) ** 2, axis=-1, keepdims=True)
            return (h - mu) * jax.lax.rsqrt(var + LN_EPS) * gamma + beta
        N = x.shape[0]
        loops = jnp.arange(N, dtype=edge_index.dtype)
        row = jnp.concatenate([edge_index[0], loops])
        col = jnp.concatenate([edge_index[1], loops])
        deg = jax.ops.segment_sum(jnp.ones(row.shape, x.dtype), col, num_segments=N)
        dinv = jnp.where(deg > 0, jax.lax.rsqrt(deg), 0.0)
        norm = dinv[row] * dinv[col]
        h = x @ W_in + b_in
        for l in range(Ws.shape[0]):
            xw = h @ Ws[l]
            msg = xw[row] * norm[:, None]
            agg = jax.ops.segment_sum(msg, col, num_segments=N) + bs[l]
            h = h + agg
            h = _layer_norm(h, gamma, beta)
            h = jax.nn.relu(h)
        return h @ W_out + b_out

    def _L2_gnn_ref(x, edge_index, W1, as1, ad1, b1, W2, as2, ad2, b2, WN, asN, adN, bN):
        import jax, jax.numpy as jnp
        import numpy as np
        N, E, H, C, IN = (50000, 15625, 4, 64, 256)

        def _gat_conv(x, src, dst, W, a_src, a_dst, b, n_nodes):
            Hh, Cc = a_src.shape
            h = (x @ W).reshape(n_nodes, Hh, Cc)
            e_src = jnp.einsum('nhc,hc->nh', h, a_src)
            e_dst = jnp.einsum('nhc,hc->nh', h, a_dst)
            e = jax.nn.leaky_relu(e_src[src] + e_dst[dst], 0.2)
            m = jax.lax.stop_gradient(jax.ops.segment_max(e, dst, num_segments=n_nodes))
            ex = jnp.exp(e - m[dst])
            denom = jax.ops.segment_sum(ex, dst, num_segments=n_nodes)
            alpha = ex / (denom[dst] + 1e-16)
            out = jax.ops.segment_sum(h[src] * alpha[:, :, None], dst, num_segments=n_nodes)
            return out.reshape(n_nodes, Hh * Cc) + b
        n = x.shape[0]
        loops = jnp.arange(n, dtype=edge_index.dtype)
        src = jnp.concatenate([edge_index[0], loops])
        dst = jnp.concatenate([edge_index[1], loops])
        inp = x
        h = jax.nn.relu(_gat_conv(x, src, dst, W1, as1, ad1, b1, n)) + inp
        h = jax.nn.relu(_gat_conv(h, src, dst, W2, as2, ad2, b2, n))
        h = _gat_conv(h, src, dst, WN, asN, adN, bN, n)
        return jax.nn.relu(h + inp)

    def _L3_gnn_ref(h, edge_index, edge_type, relation_emb, msg_w, msg_b, upd_w, upd_b, gate_w, gate_b):
        import jax, jax.numpy as jnp
        import numpy as np
        G = (1.0, 1.0)

        def to_hypercomplex(x, n_blades):
            return x.reshape(*x.shape[:-1], n_blades, -1).swapaxes(-2, -1)

        def clifford_kernel_2d(w, g):
            g0, g1 = g
            k0 = jnp.concatenate([w[0], g0 * w[1], g1 * w[2], -g0 * g1 * w[3]], axis=1)
            k1 = jnp.concatenate([w[1], w[0], -g1 * w[3], g1 * w[2]], axis=1)
            k2 = jnp.concatenate([w[2], g0 * w[3], w[0], -g0 * w[1]], axis=1)
            k3 = jnp.concatenate([w[3], w[2], w[1], w[0]], axis=1)
            return jnp.concatenate([k0, k1, k2, k3], axis=0)

        def clifford_linear(x, w, b, g=G):
            N = x.shape[0]
            k = clifford_kernel_2d(w, g)
            xf = x.swapaxes(-2, -1).reshape(N, -1)
            out = xf @ k.T + b.reshape(-1)
            C_out = w.shape[1]
            return out.reshape(N, 4, C_out).swapaxes(-2, -1)
        n_blades = 4
        num_nodes = h.shape[0]
        h_hc = to_hypercomplex(h, n_blades)
        r_hc = to_hypercomplex(relation_emb, n_blades)
        src, dst = (edge_index[0], edge_index[1])
        h_src = h_hc[src]
        r_uv = r_hc[edge_type]
        m = clifford_linear(h_src * r_uv, msg_w, msg_b)
        gate = jax.nn.sigmoid(r_uv.reshape(r_uv.shape[0], -1) @ gate_w.T + gate_b)
        m = m * gate[:, :, None]
        ones = jnp.ones_like(src, dtype=jnp.float32)
        deg_src = jax.ops.segment_sum(ones, src, num_segments=num_nodes)
        deg_dst = jax.ops.segment_sum(ones, dst, num_segments=num_nodes)
        norm = jnp.maximum(deg_src[src] * deg_dst[dst], 1.0) ** (-0.5)
        m = m * norm[:, None, None]
        h_agg = jax.ops.segment_sum(m, dst, num_segments=num_nodes)
        h_out = clifford_linear(h_hc + h_agg, upd_w, upd_b)
        return h_out.reshape(num_nodes, -1)
    edge_index = jnp.stack([src, dst])
    x = _layernorm(x + _L0_gnn_ref(x, edge_index, L0_gnn_W_layer, L0_gnn_b_layer, L0_gnn_w_a1, L0_gnn_b_a1, L0_gnn_w_a2, L0_gnn_b_a2), axis=-1)
    x = _layernorm(x + _L1_gnn_ref(x, edge_index, L1_gnn_W_in, L1_gnn_b_in, L1_gnn_Ws, L1_gnn_bs, L1_gnn_gamma, L1_gnn_beta, L1_gnn_W_out, L1_gnn_b_out), axis=-1)
    x = _layernorm(x + _L2_gnn_ref(x, edge_index, L2_gnn_W1, L2_gnn_as1, L2_gnn_ad1, L2_gnn_b1, L2_gnn_W2, L2_gnn_as2, L2_gnn_ad2, L2_gnn_b2, L2_gnn_WN, L2_gnn_asN, L2_gnn_adN, L2_gnn_bN), axis=-1)
    x = _layernorm(x + _L3_gnn_ref(x, edge_index, edge_type_500, L3_gnn_relation_emb, L3_gnn_msg_w, L3_gnn_msg_b, L3_gnn_upd_w, L3_gnn_upd_b, L3_gnn_gate_w, L3_gnn_gate_b), axis=-1)
    return x

_drawn_inputs = setup_inputs


def setup_inputs(seed=0):
    import zlib

    import numpy as np

    out = dict(_drawn_inputs(seed))
    spreads = {'L1_gnn_b_in': (0.0, 0.1),
     'L1_gnn_bs': (0.0, 0.1),
     'L1_gnn_gamma': (1.0, 0.2),
     'L1_gnn_beta': (0.0, 0.1),
     'L1_gnn_b_out': (0.0, 0.1),
     'L2_gnn_b1': (0.0, 0.462),
     'L2_gnn_b2': (0.0, 0.292),
     'L2_gnn_bN': (0.0, 0.1)}
    factors = {'L0_gnn_w_a1': 2.975,
     'L2_gnn_as1': 4.692,
     'L2_gnn_ad1': 8.0,
     'L2_gnn_ad2': 8.0,
     'L2_gnn_asN': 8.0,
     'L2_gnn_adN': 8.0,
     'L3_gnn_msg_b': 3.528,
     'L3_gnn_gate_w': 2.752}
    for name, (base, spread) in spreads.items():
        noise = np.random.default_rng([zlib.crc32(name.encode()), seed]).standard_normal(out[name].shape)
        drawn = base * np.exp(spread * noise) if base else spread * noise
        out[name] = jnp.asarray(drawn.astype(out[name].dtype))
    for name, factor in factors.items():
        out[name] = (out[name] * factor).astype(out[name].dtype)
    return out
```

```python
import numpy as np
from contextlib import ExitStack

import concourse.bass as bass
from concourse import mybir

F32 = mybir.dt.float32
BF16 = mybir.dt.bfloat16
I32 = mybir.dt.int32
ALU = mybir.AluOpType
ACT = mybir.ActivationFunctionType
AX = mybir.AxisListType

P = 128
N = 3125
E = 53125
D = 256
H = 4
R = 500
B = -(-N // P)
LAST = N - (B - 1) * P
EP, EC = 125, 425
U = 8
T = -(-((E + B * (P - 1)) // P) // U) * U
TURNS = T // U
W = D + H
NB = 5
DT = B // NB
SC_U = 17
SC_TURNS = EC // SC_U
STAGE_TURNS = (SC_TURNS - SC_TURNS // 2, SC_TURNS // 2)
assert SC_TURNS * SC_U == EC and SC_TURNS % 2 == 1
BANKS = 4
BIG = 2.0 ** 100
LN_EPS = 1e-5
GAT_EPS = 1e-16
SLOPE0, SLOPE2 = 0.01, 0.2
assert EP * EC == E and DT * NB == B and T * P >= E + B * (P - 1) - (P - 1)

CLIFFORD = [[(0, 1), (1, 1), (2, 1), (3, -1)],
            [(1, 1), (0, 1), (3, -1), (2, 1)],
            [(2, 1), (3, 1), (0, 1), (1, -1)],
            [(3, 1), (2, 1), (1, 1), (0, 1)]]

PASSES = [("degree", "dst", 1, 0), ("degree", "src", 1, 0),
          ("max", "src", 1, SLOPE0), ("attend", "src", 1, SLOPE0),
          ("plain", "dst", 1, 0), ("plain", "dst", 1, 0), ("plain", "dst", 1, 0),
          ("max", "dst", H, SLOPE2), ("attend", "dst", H, SLOPE2),
          ("max", "dst", H, SLOPE2), ("attend", "dst", H, SLOPE2),
          ("max", "dst", H, SLOPE2), ("attend", "dst", H, SLOPE2),
          ("relate", "dst", 1, 0)]
PRODUCTS = ["w_layer", "w_in", "ws0", "ws1", "ws2", "w_out", "w1", "w2", "wn", "msg", "upd"]
TURNED = {"w_layer", "msg", "upd"}
VECS = ["b_layer", "w_a1", "w_a2", "b_in", "bs0", "bs1", "bs2", "gamma", "beta", "b_out",
        "as1", "ad1", "b1", "as2", "ad2", "b2", "asn", "adn", "bn", "msg_b", "upd_b"]


def before(n, *kinds):
    return sum(k in kinds for k, _, _, _ in PASSES[:n])


class Order:

    def __init__(self, eng, sem):
        self.eng, self.sem, self.n, self.i, self.per, self.k = eng, sem, 0, None, 0, 0

    def link(self, ins):
        ins.then_inc(self.sem, 1)
        if self.i is None:
            self.n += 1
            self.eng.wait_ge(self.sem, self.n)
        else:
            self.k += 1
            self.eng.wait_ge(self.sem, self.i * self.per + (self.n + self.k))

    def enter(self, i, per):
        self.i, self.per, self.k = i, per, 0

    def leave(self, turns):
        assert self.k == self.per, (self.k, self.per)
        self.n += turns * self.per
        self.i = None


def gnn_program(nc, x, src, dst, etype, mats, vecs, scalars, relation, gate_w, clif_w, out):
    ctx = ExitStack()
    with ctx:
        def sb(name, shape, dt=F32):
            return ctx.enter_context(nc.sbuf_tensor(name, shape, dt))

        def sem(name):
            return ctx.enter_context(nc.semaphore(name))

        table = nc.dram_tensor("node_table", (B * P, D), F32).ap()
        table3 = nc.dram_tensor("node_table_scaled", (B * P, D + 1), F32).ap()
        score_table = nc.dram_tensor("score_table", (B * P, H), F32).ap()
        rel_table = nc.dram_tensor("relation_table", (R, D + 1), F32).ap()
        records = {o: nc.dram_tensor(f"records_{o}", (P * T, 4), I32).ap() for o in ("src", "dst")}

        X = sb("X", [P, B * D])
        HY = sb("HY", [P, 2 * B * D])
        Hh = HY[:, 0:B * D]
        Y = HY[:, B * D:2 * B * D]
        acc = sb("acc", [P, B * W])
        acc3 = acc[:, :].rearrange("p (b w) -> p b w", w=W)
        tmp3 = acc3[:, :, 0:D]
        rec = {o: sb(f"rec_{o}", [P, T * 4], I32) for o in ("src", "dst")}
        block_of = {o: sb(f"block_of_{o}", [P, T], I32) for o in ("src", "dst")}
        ES = sb("ES", [P, T * H])
        G = sb("G", [P, U, D + 1])
        M = sb("M", [P, U, W])
        OH = sb("OH", [P, U, P])
        OHT = sb("OHT", [P, U, P])
        NE = OHT[:, :, :].rearrange("p u n -> p (u n)").bitcast(BF16)[:, 0:U * P].rearrange("p (u n) -> p u n", n=P)
        XS = M[:, :, :].rearrange("p u d -> p (u d)")[:, 0:NB * D]
        XT = G[:, :, :].rearrange("p u d -> p (u d)")[:, 0:NB * D]
        wbuf = sb("wbuf", [P, 2, 2, D])
        wraw = sb("wraw", [P, 2, D])
        vec = {n: sb(f"v_{n}", [P, D]) for n in VECS}
        sc = sb("scal", [P, 3])
        ESN = sb("ESN", [P, B * H])
        EDM = sb("EDM", [P, B * 2 * H])
        MX = sb("MX", [P, B * H])
        edge_max = sb("edge_max", [P, H])
        SC = sb("SC", [P, U * H])
        EX = sb("EX", [P, U * H])
        exs = sb("exs", [P, B * H])
        st1 = sb("st1", [P, B])
        st2 = sb("st2", [P, B])
        deg = {o: sb(f"deg_{o}", [P, B]) for o in ("src", "dst")}
        dinv = sb("dinv", [P, B])
        ident = sb("ident", [P, P])
        ones = sb("ones", [P, P])
        before_me = sb("before_me", [P, P])
        iota_n = sb("iota_n", [P, P])
        neg_ident = sb("neg_ident", [P, H, P], BF16)
        iota_i = sb("iota_i", [P, T], I32)
        gw = sb("gw", [P, D])
        cnt = sb("cnt", [P, B])
        cnt2 = sb("cnt2", [P, B])
        cnt_i = sb("cnt_i", [P, B], I32)
        base = sb("base", [P, B])
        stage = sb("stage", [P, 2, SC_U * 4], I32)
        idx = sb("idx", [P, max(U * 4, 2 * SC_U)], I32)

        A = acc[:, :]
        S_scan = HY[0:EP, 0:B * EC]
        S_src, S_dst, S_typ, S_i, S_adr = (A[0:EP, n * EC:(n + 1) * EC].bitcast(I32) for n in range(5))
        S_q, S_f, S_pos, S_zero = (A[0:EP, (5 + n) * EC:(6 + n) * EC] for n in range(4))
        S_rec = A[0:EP, 9 * EC:13 * EC].bitcast(I32)
        S_recf = A[0:EP, 9 * EC:13 * EC]
        assert 13 * EC <= B * W
        fill = G[:, :, :].rearrange("p u d -> p (u d)")[:, 0:T * 4]
        assert T * 4 <= U * (D + 1)
        iota_t = M[:, :, :].rearrange("p u d -> p (u d)")[:, 0:T]
        bt_f = M[:, :, :].rearrange("p u d -> p (u d)")[:, T:2 * T]

        ps = ctx.enter_context(nc.psum_tensor("ps", [P, 8, 512], F32))
        psf = ps[:, :, :].rearrange("p b n -> p (b n)")
        T_ps = psf[:, 4 * 512:6 * 512]
        EDM_ps = ps[:, 6, 0:U * 2 * H]
        XT_ps = psf[:, 0:NB * D]
        Y_ps = psf[:, 3 * 512:3 * 512 + NB * D]

        s_load, s_const, s_order, s_gorder, s_aorder = sem("loaded"), sem("constants"), sem("dve_order"), sem("pool_order"), sem("act_order")
        s_cnt, s_offs, s_fill, s_filled, s_adr, s_rec = (sem(n) for n in (
            "counts_ready", "offsets_ready", "fill_ready", "filled", "addresses_ready", "records_loaded"))
        s_in, s_xs, s_xt_ps, s_xt, s_y_ps, s_y = (sem(n) for n in (
            "product_input", "xs_ready", "xt_in_psum", "xt_ready", "y_in_psum", "y_ready"))
        s_wraw, s_wT_ps, s_wT, s_kneg, s_kraw = (sem(n) for n in (
            "raw_weight_loaded", "weight_turned", "weight_ready", "clifford_signed", "clifford_loaded"))
        s_w = [sem(f"weight_loaded{k}") for k in range(2)]
        s_sorted = [sem(f"sorted{k}") for k in range(2)]
        s_idx = sem("indices_ready")
        s_sq_in, s_sq = sem("root_input"), sem("root_ready")
        s_hfree, s_relld = sem("h_free"), sem("relation_loaded")
        landed = [sem(f"landed{k}") for k in range(U)]
        rel_landed = [sem(f"rel_landed{k}") for k in range(U)]
        s_oh, s_ps, s_psfree, s_msg = (sem(n) for n in (
            "onehot_ready", "sum_in_psum", "psum_free", "message_ready"))
        s_T, s_OHT, s_edm, s_sc, s_ex = (sem(n) for n in (
            "turned_in_psum", "turned_ready", "target_scores_ready", "scores_ready", "exp_ready"))
        s_tab_sc, s_tab, s_stab_st, s_tab_st = (sem(n) for n in (
            "score_table_ready", "table_ready", "score_table_stored", "table_stored"))
        s_self, s_selfx, s_rel, s_relst, s_gz, s_gs, s_out, s_fin = (sem(n) for n in (
            "self_scores_ready", "self_exp_ready", "relation_rows_ready", "relation_stored",
            "gate_sum_ready", "gate_ready", "output_ready", "stored"))

        tab_view = table.rearrange("(b p) d -> p b d", p=P)
        tab3_view = table3.rearrange("(b p) d -> p b d", p=P)
        stab_view = score_table.rearrange("(b p) d -> p b d", p=P)
        Y3 = Y.rearrange("p (b d) -> p b d", d=D)
        H3 = Hh.rearrange("p (b d) -> p b d", d=D)
        X3 = X[:, :].rearrange("p (b d) -> p b d", d=D)
        scaled3 = acc[:, 0:B * (D + 1)].rearrange("p (b d) -> p b d", d=D + 1)
        R4 = Hh[0:EP, 0:4 * (D + 1)].rearrange("p (q d) -> p q d", d=D + 1)
        R4t = Y[0:EP, 0:4 * D].rearrange("p (q d) -> p q d", d=D)

        RAW_LOADS = 3 + 2 + len(VECS) + 3 + 1
        block = ctx.enter_context(nc.Block())

        @block.sync
        def _(sp):
            sp.dma_start(S_src, src.rearrange("(p c) -> p c", c=EC)).then_inc(s_load, 16)
            sp.dma_start(S_dst, dst.rearrange("(p c) -> p c", c=EC)).then_inc(s_load, 16)
            sp.dma_start(S_typ, etype.rearrange("(p c) -> p c", c=EC)).then_inc(s_load, 16)
            sp.wait_ge(s_const, 1)
            sp.dma_start(X3[:, 0:B - 1, :], x[0:(B - 1) * P, :].rearrange("(b p) d -> p b d", p=P)).then_inc(s_load, 16)
            sp.dma_start(X3[0:LAST, B - 1, :], x[(B - 1) * P:N, :]).then_inc(s_load, 16)
            for n in VECS:
                sp.dma_start(vec[n][:, :], vecs[n].partition_broadcast(P)).then_inc(s_load, 16)
            for n in range(3):
                sp.dma_start(sc[:, n:n + 1], scalars[n].partition_broadcast(P)).then_inc(s_load, 16)
            sp.dma_start(gw[:, :], gate_w.partition_broadcast(P)).then_inc(s_load, 16)
            sp.wait_ge(s_fill, 1)
            for o in ("src", "dst"):
                sp.dma_start(records[o].rearrange("(p t) f -> p (t f)", p=P), fill.bitcast(I32)).then_inc(s_filled, 16)
            for n, o in enumerate(("src", "dst")):
                for s_, turns in zip(s_sorted, STAGE_TURNS):
                    sp.wait_ge(s_, 16 * SC_U * turns * (n + 1))
                sp.dma_start(rec[o][:, :], records[o].rearrange("(p t) f -> p (t f)", p=P)).then_inc(s_rec, 16)

            def load_weight(j):
                name = PRODUCTS[j]
                if j >= 2:
                    sp.wait_ge(s_y_ps, 1 + DT * (j - 1))
                if name in ("msg", "upd"):
                    sp.wait_ge(s_wT_ps, 1 if name == "msg" else 2)
                    for i in range(4):
                        for jj, (w, _) in enumerate(CLIFFORD[i]):
                            sp.dma_start(wraw[64 * (i % 2):64 * (i % 2) + 64, i // 2, 64 * jj:64 * jj + 64],
                                         clif_w[name][w, :, :]).then_inc(s_kraw, 16)
                elif name in TURNED:
                    sp.dma_start(wraw[:, :, :], mats[name].rearrange("(k p) n -> p k n", p=P)).then_inc(s_wraw, 16)
                else:
                    sp.dma_start(wbuf[:, j % 2, :, :], mats[name].rearrange("(k p) n -> p k n", p=P)).then_inc(s_w[j % 2], 16)

            def store_tables(stage):
                sp.wait_ge(s_tab_sc, stage)
                sp.dma_start(stab_view, ESN[:, :].rearrange("p (b h) -> p b h", h=H)).then_inc(s_stab_st, 16)

            load_weight(0)
            load_weight(1)
            score_stage = 0
            for n in range(7):
                j = (0, 2, 3, 4, 6, 7, 8)[n]
                if n == 0 or n >= 4:
                    score_stage += 1
                    store_tables(score_stage)
                sp.wait_ge(s_tab, n + 1)
                sp.dma_start(tab_view, Y3).then_inc(s_tab_st, 16)
                for jj in {0: (2,), 1: (3,), 2: (4,), 3: (5, 6), 4: (7,), 5: (8,), 6: (9,)}[n]:
                    load_weight(jj)
            sp.wait_ge(s_hfree, 1)
            sp.dma_start(R4[:, :, 0:D], relation.rearrange("(q p) d -> p q d", p=EP)).then_inc(s_relld, 16)
            sp.wait_ge(s_rel, 1)
            sp.dma_start(rel_table.rearrange("(q p) d -> p q d", p=EP), R4).then_inc(s_relst, 16)
            sp.wait_ge(s_tab, 8)
            sp.dma_start(tab3_view, scaled3).then_inc(s_tab_st, 16)
            load_weight(10)
            sp.wait_ge(s_out, 1)
            sp.dma_start(out[0:(B - 1) * P, :].rearrange("(b p) d -> p b d", p=P), X3[:, 0:B - 1, :]).then_inc(s_fin, 16)
            sp.dma_start(out[(B - 1) * P:N, :], X3[0:LAST, B - 1, :]).then_inc(s_fin, 16)
            sp.wait_ge(s_fin, 32)

        @block.gpsimd
        def _(pool):
            order = Order(pool, s_gorder)
            pool.memset(X3[:, B - 1, :], 0.0).then_inc(s_const, 1)
            order.link(pool.memset(ident[:, :], 0.0))
            order.link(pool.affine_select(out=ident[:, :], in_=ident[:, :], compare_op=ALU.not_equal, fill=1.0,
                                          base=0, pattern=[[-1, P]], channel_multiplier=1))
            order.link(pool.memset(ones[:, :], 1.0))
            order.link(pool.affine_select(out=before_me[:, :], in_=ones[:, :], compare_op=ALU.is_gt, fill=0.0,
                                          base=0, pattern=[[1, P]], channel_multiplier=-1))
            pool.iota(iota_i[:, :], pattern=[[1, T]], base=0, channel_multiplier=0).then_inc(s_const, 1)

            pool.wait_ge(s_filled, 32)
            for n, o in enumerate(("src", "dst")):
                pool.wait_ge(s_adr, n + 1)

                def turn(t, st, past):
                    served = STAGE_TURNS[st] * n + past
                    if not (isinstance(served, int) and served == 0):
                        pool.wait_ge(s_sorted[st], served * (16 * SC_U))
                    pool.tensor_copy(idx[0:EP, st * SC_U:(st + 1) * SC_U], S_adr[:, bass.ds(t * SC_U, SC_U)]).then_inc(s_idx, 1)
                    pool.tensor_copy(stage[0:EP, st, :], S_rec[:, bass.ds(t * (SC_U * 4), SC_U * 4)]).then_inc(s_idx, 1)
                    pool.wait_ge(s_idx, t * 2 + (2 * n * SC_TURNS + 2))
                    pool.nop(nofuse=True)
                    for k in range(SC_U):
                        pool.indirect_dma_start(
                            out=records[o][:, :],
                            out_offset=bass.IndirectOffsetOnAxis(ap=idx[0:EP, st * SC_U + k:st * SC_U + k + 1], axis=0),
                            in_=stage[0:EP, st, 4 * k:4 * k + 4], in_offset=None).then_inc(s_sorted[st], 16)

                turn(0, 0, 0)
                turn(1, 1, 0)
                turn(2, 0, 1)
                with pool.Fori(0, (SC_TURNS - 3) // 2) as i:
                    turn(i * 2 + 3, 1, i + 1)
                    turn(i * 2 + 4, 0, i + 2)

            def gather(n, dest, tab, col, sems, use):
                o = PASSES[n][1]
                with pool.Fori(0, TURNS) as i:
                    for half in range(2):
                        own = range(half * U // 2, (half + 1) * U // 2)
                        pool.wait_ge(s_psfree, i * U + (BANKS + n * T + own[-1] + 1 - U))
                        part = idx[:, half * U * 2:(half + 1) * U * 2]
                        pool.tensor_copy(part, rec[o][:, bass.ds((i * 2 + half) * (U * 2), U * 2)]).then_inc(s_idx, 1)
                        pool.wait_ge(s_idx, i * 2 + (4 * SC_TURNS + 2 * use * TURNS + half + 1))
                        pool.nop(nofuse=True)
                        for k in own:
                            pool.wait_ge(s_psfree, i * U + (BANKS + n * T + k + 1 - U))
                            pool.nop(nofuse=True)
                            for d_, t_, c_, s_ in zip(dest, tab, col, sems):
                                pool.indirect_dma_start(
                                    out=d_(k), out_offset=None, in_=t_,
                                    in_offset=bass.IndirectOffsetOnAxis(
                                        ap=idx[:, k * 4 + c_:k * 4 + c_ + 1], axis=0)).then_inc(s_[k], 16)

            pool.wait_ge(s_rec, 32)
            tables = scores = 0
            for n, (kind, o, heads, _) in enumerate(PASSES):
                use = before(n, "max", "attend", "plain", "relate")
                if kind == "max":
                    scores += 1
                    pool.wait_ge(s_stab_st, 16 * scores)
                    gather(n, [lambda k: G[:, k, 0:H]], [score_table[:, :]], [0], [landed], use)
                elif kind in ("attend", "plain"):
                    tables += 1
                    pool.wait_ge(s_tab_st, 16 * tables)
                    gather(n, [lambda k: G[:, k, 0:D]], [table[:, :]], [0], [landed], use)
                elif kind == "relate":
                    pool.wait_ge(s_tab_st, 16 * (tables + 1))
                    pool.wait_ge(s_relst, 16)
                    gather(n, [lambda k: G[:, k, :], lambda k: M[:, k, 0:D + 1]], [table3[:, :], rel_table[:, :]],
                           [0, 2], [landed, rel_landed], use)

        @block.tensor
        def _(pe):
            def offsets(n):
                pe.wait_ge(s_const, 2)
                pe.wait_ge(s_cnt, n + 1)
                nc.tensor.matmul(ps[0:EP, 0, 0:B], before_me[0:EP, 0:EP], cnt[0:EP, :], start=True, stop=True)
                nc.tensor.matmul(ps[:, 1, 0:B], ones[0:EP, :], cnt[0:EP, :], start=True, stop=True).then_inc(s_offs, 1)

            turned = [0]

            def turn_weight(j):
                name = PRODUCTS[j]
                if name not in TURNED:
                    return
                if name == "w_layer":
                    pe.wait_ge(s_wraw, 16)
                else:
                    pe.wait_ge(s_kneg, turned[0])
                for k in range(2):
                    for m in range(2):
                        last = nc.tensor.transpose(ps[:, 6 + k, m * P:(m + 1) * P], wraw[:, m, k * P:(k + 1) * P], ident[:, :])
                last.then_inc(s_wT_ps, 1)
                turned[0] += 1

            loaded = [0, 0]

            def product(j):
                turn_weight(j)
                if PRODUCTS[j] in TURNED:
                    pe.wait_ge(s_wT, turned[0])
                else:
                    loaded[j % 2] += 1
                    pe.wait_ge(s_w[j % 2], 16 * loaded[j % 2])
                with pe.Fori(0, DT) as i:
                    pe.wait_ge(s_xs, i + (DT * j + 1))
                    for q in range(2 * NB):
                        last = nc.tensor.transpose(XT_ps[:, q * P:(q + 1) * P], XS[:, q * P:(q + 1) * P], ident[:, :])
                    last.then_inc(s_xt_ps, 1)
                    pe.wait_ge(s_xt, i + (DT * j + 1))
                    pe.wait_ge(s_y, i + (1 + DT * j))
                    for q in range(NB):
                        for k in range(2):
                            last = nc.tensor.matmul(Y_ps[:, q * D:(q + 1) * D], XT[:, (2 * q + k) * P:(2 * q + k + 1) * P],
                                                    wbuf[:, j % 2, k, :], start=(k == 0), stop=(k == 1))
                    last.then_inc(s_y_ps, 1)

            def tile_pass(n):
                kind, o, heads, _ = PASSES[n]
                use = before(n, "max", "attend", "plain", "relate")
                att, msg = before(n, "attend"), before(n, "attend", "relate")
                with pe.Fori(0, TURNS) as i:
                    pe.wait_ge(s_oh, i + (n * TURNS + 1))
                    if kind == "attend":
                        for k in range(U):
                            last = nc.tensor.transpose(T_ps[:, k * P:(k + 1) * P], OH[:, k, :], ident[:, :])
                        last.then_inc(s_T, 1)
                        pe.wait_ge(s_OHT, i + (att * TURNS + 1))
                        for k in range(U):
                            b = pe.value_load(block_of[o][0:1, bass.ds(i * U + k, 1)], min_val=0, max_val=B - 1)
                            last = nc.tensor.matmul(EDM_ps[:, k * 2 * H:(k + 1) * 2 * H], OHT[:, k, :],
                                                    EDM[:, bass.ds(b * (2 * H), 2 * H)], start=True, stop=True)
                        last.then_inc(s_edm, 1)
                    for k in range(U):
                        bank = k % BANKS
                        pe.wait_ge(s_psfree, i * U + (n * T + k + 1))
                        if kind == "degree":
                            last = nc.tensor.matmul(ps[:, bank, 0:1], OH[:, k, :], ones[:, 0:1], start=True, stop=True)
                        elif kind == "max":
                            pe.wait_ge(landed[k], i * 16 + 16 * (use * TURNS + 1))
                            nc.tensor.matmul(ps[:, bank, 0:heads * P], NE[:, k, :],
                                             neg_ident[:, 0:heads, :], start=True, stop=False)
                            for h in range(heads):
                                last = nc.tensor.matmul(ps[:, bank, h * P:(h + 1) * P], G[:, k, h:h + 1].to_broadcast([P, P]),
                                                        ident[:, :], start=False, stop=(h == heads - 1))
                        elif kind == "plain":
                            pe.wait_ge(landed[k], i * 16 + 16 * (use * TURNS + 1))
                            last = nc.tensor.matmul(ps[:, bank, 0:D], OH[:, k, :], G[:, k, 0:D], start=True, stop=True)
                        else:
                            pe.wait_ge(s_msg, i * U + (msg * T + k + 1))
                            w = W if heads == H else D + 1
                            last = nc.tensor.matmul(ps[:, bank, 0:w], OH[:, k, :], M[:, k, 0:w], start=True, stop=True)
                        last.then_inc(s_ps, 1)

            offsets(0)
            offsets(1)
            for step in PLAN:
                product(step[1]) if step[0] == "product" else tile_pass(step[1]) if step[0] == "pass" else None

        @block.scalar
        def _(act):
            turned = [0]

            def product(j):
                name = PRODUCTS[j]
                if name in TURNED:
                    if name != "w_layer":
                        act.wait_ge(s_kraw, 16 * 16 * turned[0])
                        negs = [(i, jj) for i in range(4) for jj in range(4) if CLIFFORD[i][jj][1] < 0]
                        for i, jj in negs:
                            w = wraw[64 * (i % 2):64 * (i % 2) + 64, i // 2, 64 * jj:64 * jj + 64]
                            last = nc.scalar.mul(w, w, -1.0)
                        last.then_inc(s_kneg, 1)
                    turned[0] += 1
                    act.wait_ge(s_wT_ps, turned[0])
                    nc.scalar.copy(wbuf[:, j % 2, :, :], ps[:, 6:8, 0:D]).then_inc(s_wT, 1)
                act.wait_ge(s_in, j + 1)
                source = X if name in ("w_layer", "w_in", "w1") else HY
                with act.Fori(0, DT) as i:
                    act.wait_ge(s_xt_ps, i + (1 + DT * j))
                    nc.scalar.copy(XS, source[:, bass.ds(i * (NB * D), NB * D)]).then_inc(s_xs, 1)
                    act.wait_ge(s_xt_ps, i + (1 + DT * j + 1))
                    act.wait_ge(s_y_ps, i + (1 + DT * j))
                    nc.scalar.copy(XT, XT_ps).then_inc(s_xt, 1)

            def tile_pass(n):
                if PASSES[n][0] != "attend":
                    return
                att = before(n, "attend")
                with act.Fori(0, TURNS) as i:
                    act.wait_ge(s_T, i + (att * TURNS + 1))
                    nc.scalar.copy(OHT[:, :, :].rearrange("p u n -> p (u n)"), T_ps).then_inc(s_OHT, 1)
                    act.wait_ge(s_sc, i + (att * TURNS + 1))
                    nc.scalar.activation(EX[:, :], SC[:, :], ACT.Exp).then_inc(s_ex, 1)

            n_self = roots = 0
            for step in PLAN:
                if step[0] == "product":
                    product(step[1])
                elif step[0] == "pass":
                    tile_pass(step[1])
                elif step[0] == "self":
                    n_self += 1
                    act.wait_ge(s_self, n_self)
                    nc.scalar.activation(exs[:, :], exs[:, :], ACT.Exp).then_inc(s_selfx, 1)
                elif step[0] == "root":
                    roots += 1
                    act.wait_ge(s_sq_in, roots)
                    nc.scalar.activation(st2[:, :], st2[:, :], ACT.Sqrt).then_inc(s_sq, 1)
                elif step[0] == "gate":
                    act.wait_ge(s_gz, 1)
                    nc.scalar.activation(cnt[0:EP, 0:4], cnt[0:EP, 0:4], ACT.Exp, scale=-1.0).then_inc(s_gs, 1)

        @block.vector
        def _(dve):
            order = Order(dve, s_order)
            L = order.link
            v = nc.vector
            nb = lambda ap, w=D: ap.unsqueeze(2).to_broadcast([P, B, w])
            vb = lambda ap: ap.unsqueeze(1).to_broadcast([P, B, D])

            def sort(n, o):
                key, other = (S_src, S_dst) if o == "src" else (S_dst, S_src)
                if n:
                    for s_, turns in zip(s_sorted, STAGE_TURNS):
                        dve.wait_ge(s_, 16 * SC_U * turns * n)
                L(v.tensor_scalar(S_i, key, 7, None, ALU.logical_shift_right))
                L(v.tensor_copy(S_q, S_i))
                L(v.tensor_scalar(S_i, key, P - 1, None, ALU.bitwise_and))
                r = S_rec.rearrange("p (c f) -> p c f", f=4)
                v.tensor_copy(S_recf.rearrange("p (c f) -> p c f", f=4)[:, :, 1:2], S_i.unsqueeze(2))
                v.tensor_copy(r[:, :, 0:1], other.unsqueeze(2))
                v.tensor_copy(r[:, :, 2:3], S_typ.unsqueeze(2))
                v.memset(r[:, :, 3:4], 0)
                L(v.memset(S_zero, 0.0))
                with dve.Fori(0, B) as b:
                    order.enter(b, 2)
                    L(v.tensor_scalar(S_f, S_q, iota_n[0:EP, bass.ds(b, 1)], None, ALU.is_equal))
                    L(v.tensor_tensor_scan(S_scan[:, bass.ds(b * EC, EC)], S_f, S_zero, 0.0, ALU.add, ALU.add))
                    order.leave(B)
                scan3 = S_scan.rearrange("p (b c) -> p b c", c=EC)
                v.tensor_copy(cnt[0:EP, :].unsqueeze(2), scan3[:, :, EC - 1:EC]).then_inc(s_cnt, 1)
                dve.wait_ge(s_offs, n + 1)
                L(v.tensor_scalar(cnt_i[:, :], ps[:, 1, 0:B], float(P - 1), None, ALU.add))
                L(v.tensor_scalar(cnt_i[:, :], cnt_i[:, :], 7, None, ALU.logical_shift_right))
                L(v.tensor_copy(cnt2[:, :], cnt_i[:, :]))
                L(v.tensor_tensor_scan(base[:, :], cnt2[:, :], nul_b, 0.0, ALU.add, ALU.add))
                L(v.tensor_tensor(cnt2[:, :], base[:, :], cnt2[:, :], ALU.subtract))
                L(v.scalar_tensor_tensor(base[0:EP, :], cnt2[0:EP, :], float(P), ps[0:EP, 0, 0:B], ALU.mult, ALU.add))
                L(v.tensor_scalar(base[0:EP, :], base[0:EP, :], -1.0, None, ALU.add))
                L(v.tensor_tensor(scan3, scan3, base[0:EP, :].unsqueeze(2).to_broadcast([EP, B, EC]), ALU.add))
                L(v.memset(S_pos, 0.0))
                with dve.Fori(0, B) as b:
                    order.enter(b, 2)
                    L(v.scalar_tensor_tensor(S_f, S_q, iota_n[0:EP, bass.ds(b, 1)], S_scan[:, bass.ds(b * EC, EC)],
                                             ALU.is_equal, ALU.mult))
                    L(v.tensor_tensor(S_pos, S_pos, S_f, ALU.add))
                    order.leave(B)
                L(v.tensor_copy(S_adr, S_pos))
                L(v.tensor_scalar(S_i, S_adr, P - 1, None, ALU.bitwise_and))
                L(v.tensor_scalar(S_adr, S_adr, 7, None, ALU.logical_shift_right))
                L(v.tensor_copy(S_f, S_i))
                L(v.tensor_copy(S_pos, S_adr))
                L(v.scalar_tensor_tensor(S_f, S_f, float(T), S_pos, ALU.mult, ALU.add))
                v.tensor_copy(S_adr, S_f).then_inc(s_adr, 1)
                L(v.memset(bt_f, 0.0))
                with dve.Fori(0, B - 1) as b:
                    order.enter(b, 1)
                    L(v.scalar_tensor_tensor(bt_f, iota_t, cnt2[:, bass.ds(b + 1, 1)], bt_f, ALU.is_ge, ALU.add))
                    order.leave(B - 1)
                L(v.tensor_copy(block_of[o][:, :], bt_f))

            def product(j, finish):
                with dve.Fori(0, DT) as i:
                    dve.wait_ge(s_y_ps, i + (1 + DT * j + 1))
                    finish(Y if j != 1 else Hh, i).then_inc(s_y, 1)
                dve.wait_ge(s_y, 1 + DT * (j + 1))

            def add_bias(name):
                def f(where, i):
                    return v.tensor_tensor(where[:, bass.ds(i * (NB * D), NB * D)].rearrange("p (b d) -> p b d", d=D),
                                           Y_ps.rearrange("p (b d) -> p b d", d=D),
                                           vec[name][:, :].unsqueeze(1).to_broadcast([P, NB, D]), ALU.add)
                return f

            def scaled(where, i):
                return v.tensor_tensor(where[:, bass.ds(i * (NB * D), NB * D)].rearrange("p (b d) -> p b d", d=D),
                                       Y_ps.rearrange("p (b d) -> p b d", d=D),
                                       dinv[:, bass.ds(i * NB, NB)].unsqueeze(2).to_broadcast([P, NB, D]), ALU.mult)

            def copied(where, i):
                return v.tensor_copy(where[:, bass.ds(i * (NB * D), NB * D)], Y_ps)

            def tile_pass(n):
                kind, o, heads, slope = PASSES[n]
                use = before(n, "max", "attend", "plain", "relate")
                att = before(n, "attend")
                where = {"degree": (deg[o], 1, 1), "max": (MX, H, heads), "plain": (acc, W, D)}.get(
                    kind, (acc, W, W if heads == H else D + 1))
                dloc = rec[o][:, :].bitcast(F32)
                links = {"degree": 0, "max": U, "plain": 0, "relate": 0, "attend": 4}[kind]
                with dve.Fori(0, TURNS) as i:
                    order.enter(i, links)
                    local = dloc[:, bass.ds(i * (U * 4), U * 4)].rearrange("p (u f) -> p u f", f=4)[:, :, 1:2].to_broadcast([P, U, P])
                    cols = iota_n[:, :].unsqueeze(1).to_broadcast([P, U, P])
                    v.tensor_tensor(NE if kind == "max" else OH[:, :, :], cols, local,
                                    ALU.not_equal if kind == "max" else ALU.is_equal).then_inc(s_oh, 1)
                    if kind == "attend":
                        dve.wait_ge(s_edm, i + (att * TURNS + 1))
                        edm = EDM_ps.rearrange("p (u s h) -> p u s h", u=U, h=H)
                        s3 = SC[:, :].rearrange("p (u h) -> p u h", h=H)
                        L(v.tensor_tensor(s3, ES[:, bass.ds(i * (U * H), U * H)].rearrange("p (u h) -> p u h", h=H),
                                          edm[:, :, 0, :], ALU.add))
                        L(v.scalar_tensor_tensor(SC[:, :], SC[:, :], slope, SC[:, :], ALU.mult, ALU.max))
                        L(v.tensor_tensor(s3, s3, edm[:, :, 1, :], ALU.subtract))
                        v.tensor_scalar(SC[:, :], SC[:, :], 0.0, None, ALU.min).then_inc(s_sc, 1)
                        dve.wait_ge(s_ex, i + (att * TURNS + 1))
                        L(v.tensor_copy(M[:, :, D:D + H], EX[:, :].rearrange("p (u h) -> p u h", h=H)))

                    def message(k):
                        dve.wait_ge(landed[k], i * 16 + 16 * (use * TURNS + 1))
                        if kind == "relate":
                            dve.wait_ge(rel_landed[k], i * 16 + 16)
                            ins = v.tensor_tensor(M[:, k, 0:D + 1], M[:, k, 0:D + 1], G[:, k, :], ALU.mult)
                        elif heads == 1:
                            ins = v.tensor_scalar(M[:, k, 0:D], G[:, k, 0:D], EX[:, k * H:k * H + 1], None, ALU.mult)
                        else:
                            ins = v.tensor_tensor(M[:, k, 0:D].rearrange("p (h c) -> p h c", h=H),
                                                  G[:, k, 0:D].rearrange("p (h c) -> p h c", h=H),
                                                  EX[:, k * H:(k + 1) * H].unsqueeze(2).to_broadcast([P, H, D // H]), ALU.mult)
                        ins.then_inc(s_msg, 1)

                    def drain(k):
                        b = dve.value_load(block_of[o][0:1, bass.ds(i * U + k, 1)], min_val=0, max_val=B - 1)
                        dve.wait_ge(s_ps, i * U + (n * T + k + 1))
                        dve.wait_ge(s_psfree, i * U + (BANKS + n * T + k))
                        full, stride, w = where
                        part = full[:, bass.ds(b * stride, w)]
                        if kind == "max":
                            L(v.tensor_reduce(edge_max[:, 0:heads], ps[:, k % BANKS, 0:heads * P].rearrange("p (h e) -> p h e", h=heads),
                                              AX.X, ALU.max))
                            v.tensor_copy(ES[:, bass.ds((i * U + k) * H, H)], G[:, k, 0:H])
                            ins = v.tensor_tensor(part, part, edge_max[:, 0:heads], ALU.max)
                        else:
                            ins = v.tensor_tensor(part, part, ps[:, k % BANKS, 0:w], ALU.add)
                        ins.then_inc(s_psfree, 1)

                    if kind in ("attend", "relate"):
                        message(0)
                        for k in range(1, U):
                            message(k)
                            drain(k - 1)
                        drain(U - 1)
                    else:
                        for k in range(U):
                            drain(k)
                    order.leave(TURNS)
                L(v.memset(st1[:, :], 0.0))

            roots = [0]

            def inverse_root(dest):
                roots[0] += 1
                dve.wait_ge(s_sq, roots[0])
                L(v.reciprocal(dest[:, :], st2[:, :]))

            def layer_norm(a3, tmp, gamma=None, beta=None):
                L(v.tensor_reduce(st1[:, :], a3, AX.X, ALU.add))
                L(v.tensor_scalar(st1[:, :], st1[:, :], 1.0 / D, None, ALU.mult))
                L(v.tensor_tensor(a3, a3, nb(st1[:, :]), ALU.subtract))
                L(v.tensor_tensor(tmp, a3, a3, ALU.mult))
                L(v.tensor_reduce(st2[:, :], tmp, AX.X, ALU.add))
                v.tensor_scalar(st2[:, :], st2[:, :], 1.0 / D, LN_EPS, ALU.mult, ALU.add).then_inc(s_sq_in, 1)
                inverse_root(st2)
                L(v.tensor_tensor(a3, a3, nb(st2[:, :]), ALU.mult))
                if gamma is not None:
                    L(v.tensor_tensor(a3, a3, vb(gamma), ALU.mult))
                    L(v.tensor_tensor(a3, a3, vb(beta), ALU.add))

            EDM4 = EDM[:, :].rearrange("p (b s h) -> p b s h", s=2, h=H)
            ESN3 = ESN[:, :].rearrange("p (b h) -> p b h", h=H)
            MX3 = MX[:, :].rearrange("p (b h) -> p b h", h=H)
            exs3 = exs[:, :].rearrange("p (b h) -> p b h", h=H)

            def score(dest, a, heads):
                L(v.tensor_tensor(tmp3, Y3, vb(a), ALU.mult))
                c = D // heads
                for h in range(heads):
                    L(v.tensor_reduce(dest(h), tmp3[:, :, h * c:(h + 1) * c], AX.X, ALU.add))

            def maxima(slope):
                m = EDM4[:, :, 1, :]
                L(v.tensor_tensor(m, MX3, EDM4[:, :, 0, :], ALU.add))
                L(v.scalar_tensor_tensor(m, m, slope, m, ALU.mult, ALU.max))

            nul_b = exs[:, 0:B]
            dve.wait_ge(s_const, 2)
            v.memset(exs[:, :], 0.0)
            v.memset(ESN[:, :], 0.0)
            v.memset(EDM[:, :], 0.0)
            v.memset(edge_max[:, :], 0.0)
            v.memset(deg["src"][:, :], 0.0)
            v.memset(deg["dst"][:, :], 0.0)
            v.tensor_copy(iota_n[:, :], iota_i[:, 0:P])
            v.tensor_copy(iota_t, iota_i[:, :])
            L(v.memset(fill, 0.0))
            v.memset(fill.rearrange("p (t f) -> p t f", f=4)[:, :, 1:2], -1.0).then_inc(s_fill, 1)
            dve.sem_inc(s_psfree, BANKS)
            for s in (s_y, s_y_ps, s_xt_ps):
                dve.sem_inc(s, 1)
            dve.wait_ge(s_load, 16 * RAW_LOADS)
            for h in range(H):
                L(v.tensor_scalar(neg_ident[:, h, :], ident[:, :], -BIG, None, ALU.mult))
            sort(0, "src")
            sort(1, "dst")
            dve.wait_ge(s_rec, 32)
            tables = [0]

            def table_ready(ins):
                ins.then_inc(s_tab, 1)

            def attention(scale_first, n_max, n_att, heads, slope, src_vec, dst_vec, self_loop):
                score(lambda h: ESN3[:, :, h:h + 1], vec[src_vec][:, :], heads)
                if not self_loop:
                    L(v.tensor_scalar(ESN3[:, :, 0:1], ESN3[:, :, 0:1], sc[:, 1:2], None, ALU.add))
                v.tensor_copy(exs[:, :], ESN[:, :]).then_inc(s_tab_sc, 1)
                score(lambda h: EDM4[:, :, 0, h:h + 1], vec[dst_vec][:, :], heads)
                if not self_loop:
                    L(v.tensor_scalar(EDM4[:, :, 0, 0:1], EDM4[:, :, 0, 0:1], sc[:, 0:1], None, ALU.add))
                if self_loop:
                    L(v.tensor_copy(MX[:, :], ESN[:, :]))
                else:
                    L(v.memset(MX[:, :], -BIG))
                tile_pass(n_max)
                maxima(slope)
                L(v.memset(acc[:, :], 0.0))
                tile_pass(n_att)
                if self_loop:
                    L(v.tensor_tensor(exs3, ESN3, EDM4[:, :, 0, :], ALU.add))
                    L(v.scalar_tensor_tensor(exs[:, :], exs[:, :], slope, exs[:, :], ALU.mult, ALU.max))
                    v.tensor_tensor(exs3, exs3, EDM4[:, :, 1, :], ALU.subtract).then_inc(s_self, 1)

            n_self = 0
            n_tab = 0
            for step in PLAN:
                what = step[0]
                if what == "degrees":
                    tile_pass(0)
                    tile_pass(1)
                    v.tensor_scalar(st2[:, :], deg["dst"][:, :], 1.0, None, ALU.add).then_inc(s_sq_in, 1)
                    inverse_root(dinv)
                elif what == "L0":
                    dve.sem_inc(s_in, 1)
                    product(0, add_bias("b_layer"))
                    dve.sem_inc(s_tab, 1)
                    attention(False, 2, 3, 1, SLOPE0, "w_a2", "w_a1", False)
                    den = acc3[:, :, D:D + 1]
                    L(v.tensor_scalar(den, den, 1e-30, None, ALU.max))
                    L(v.reciprocal(st1[:, :].unsqueeze(2), den))
                    L(v.tensor_tensor(tmp3, tmp3, nb(st1[:, :]), ALU.mult))
                    L(v.tensor_tensor(X3, X3, tmp3, ALU.add))
                    layer_norm(X3, tmp3)
                    dve.sem_inc(s_in, 1)
                elif what == "L1in":
                    product(1, add_bias("b_in"))
                elif what == "conv":
                    l = step[1]
                    dve.sem_inc(s_in, 1)
                    product(2 + l, scaled)
                    dve.sem_inc(s_tab, 1)
                    L(v.memset(acc[:, :], 0.0))
                    tile_pass(4 + l)
                    L(v.tensor_tensor(tmp3, tmp3, Y3, ALU.add))
                    L(v.tensor_tensor(tmp3, tmp3, nb(dinv[:, :]), ALU.mult))
                    L(v.tensor_tensor(tmp3, tmp3, vb(vec[f"bs{l}"][:, :]), ALU.add))
                    L(v.tensor_tensor(H3, H3, tmp3, ALU.add))
                    layer_norm(H3, tmp3, vec["gamma"][:, :], vec["beta"][:, :])
                    L(v.tensor_scalar(Hh, Hh, 0.0, None, ALU.max))
                elif what == "L1out":
                    dve.sem_inc(s_in, 1)
                    product(5, add_bias("b_out"))
                    L(v.tensor_tensor(X3, X3, Y3, ALU.add))
                    layer_norm(X3, tmp3)
                elif what == "gat":
                    l = step[1]
                    dve.sem_inc(s_in, 1)
                    product(6 + l, copied)
                    dve.sem_inc(s_tab, 1)
                    sfx = ("1", "2", "n")[l]
                    attention(True, 7 + 2 * l, 8 + 2 * l, H, SLOPE2, "as" + sfx, "ad" + sfx, True)
                elif what == "self":
                    l = step[1]
                    n_self += 1
                    dve.wait_ge(s_selfx, n_self)
                    den = acc3[:, :, D:W]
                    L(v.tensor_tensor(den, den, exs3, ALU.add))
                    L(v.tensor_scalar(den, den, GAT_EPS, None, ALU.add))
                    c = D // H
                    for h in range(H):
                        yh, ah = Y3[:, :, h * c:(h + 1) * c], acc3[:, :, h * c:(h + 1) * c]
                        L(v.tensor_tensor(yh, yh, exs3[:, :, h:h + 1].to_broadcast([P, B, c]), ALU.mult))
                        L(v.tensor_tensor(ah, ah, yh, ALU.add))
                    L(v.reciprocal(exs3, den))
                    for h in range(H):
                        ah = acc3[:, :, h * c:(h + 1) * c]
                        L(v.tensor_tensor(ah, ah, exs3[:, :, h:h + 1].to_broadcast([P, B, c]), ALU.mult))
                    L(v.tensor_tensor(H3, tmp3, vb(vec[("b1", "b2", "bn")[l]][:, :]), ALU.add))
                    if l == 2:
                        L(v.tensor_tensor(Hh, Hh, X[:, :], ALU.add))
                    L(v.tensor_scalar(Hh, Hh, 0.0, None, ALU.max))
                    if l != 1:
                        if l == 0:
                            L(v.tensor_tensor(Hh, Hh, X[:, :], ALU.add))
                        else:
                            L(v.tensor_tensor(X[:, :], Hh, X[:, :], ALU.add))
                            layer_norm(X3, tmp3)
                elif what == "gate":
                    dve.sem_inc(s_hfree, 1)
                    dve.wait_ge(s_relld, 16)
                    gr = R4[:, :, 0:D].rearrange("p q (k c) -> p q k c", k=4)
                    gwr = gw[0:EP, :].rearrange("p (c k) -> p k c", k=4)
                    for q in range(4):
                        L(v.tensor_tensor(R4t[:, q, :].rearrange("p (k c) -> p k c", k=4), gr[:, q, :, :], gwr, ALU.mult))
                    L(v.tensor_reduce(cnt[0:EP, 0:4], R4t, AX.X, ALU.add))
                    v.tensor_scalar(cnt[0:EP, 0:4], cnt[0:EP, 0:4], sc[0:EP, 2:3], None, ALU.add).then_inc(s_gz, 1)
                    dve.wait_ge(s_gs, 1)
                    L(v.tensor_scalar(cnt[0:EP, 0:4], cnt[0:EP, 0:4], 1.0, None, ALU.add))
                    L(v.reciprocal(cnt[0:EP, 0:4], cnt[0:EP, 0:4]))
                    L(v.tensor_tensor(R4[:, :, 0:D], R4[:, :, 0:D],
                                      cnt[0:EP, 0:4].unsqueeze(2).to_broadcast([EP, 4, D]), ALU.mult))
                    v.tensor_copy(R4[:, :, D:D + 1], cnt[0:EP, 0:4].unsqueeze(2)).then_inc(s_rel, 1)
                elif what == "relate":
                    v.tensor_scalar(st2[:, :], deg["src"][:, :], 1.0, None, ALU.max).then_inc(s_sq_in, 1)
                    inverse_root(dinv)
                    L(v.tensor_tensor(scaled3[:, :, 0:D], X3, nb(dinv[:, :]), ALU.mult))
                    v.tensor_copy(scaled3[:, :, D:D + 1], dinv[:, :].unsqueeze(2)).then_inc(s_tab, 1)
                    dve.wait_ge(s_tab_st, 16 * 8)
                    L(v.memset(acc[:, :], 0.0))
                    tile_pass(13)
                    dve.wait_ge(s_relst, 16)
                    v.tensor_scalar(st2[:, :], deg["dst"][:, :], 1.0, None, ALU.max).then_inc(s_sq_in, 1)
                    inverse_root(dinv)
                    L(v.tensor_tensor(H3, tmp3, nb(dinv[:, :]), ALU.mult))
                    dve.sem_inc(s_in, 1)
                    L(v.tensor_tensor(st2[:, :].unsqueeze(2), acc3[:, :, D:D + 1], dinv[:, :].unsqueeze(2), ALU.mult))
                    L(v.tensor_tensor(tmp3, vb(vec["msg_b"][:, :]), nb(st2[:, :]), ALU.mult))
                    product(9, copied)
                    L(v.tensor_tensor(H3, X3, Y3, ALU.add))
                    L(v.tensor_tensor(H3, H3, tmp3, ALU.add))
                    dve.sem_inc(s_in, 1)
                    product(10, add_bias("upd_b"))
                    for k in range(4):
                        xk = X[:, :].rearrange("p (n k) -> p n k", k=4)[:, :, k:k + 1].rearrange("p (b c) k -> p b (c k)", c=D // 4)
                        L(v.tensor_tensor(xk, xk, Y3[:, :, k * (D // 4):(k + 1) * (D // 4)], ALU.add))
                    layer_norm(X3, tmp3)
                    dve.sem_inc(s_out, 1)


PLAN = [("degrees",), ("pass", 0), ("pass", 1), ("root",),
        ("L0",), ("product", 0), ("pass", 2), ("pass", 3), ("root",),
        ("L1in",), ("product", 1),
        ("conv", 0), ("product", 2), ("pass", 4), ("root",),
        ("conv", 1), ("product", 3), ("pass", 5), ("root",),
        ("conv", 2), ("product", 4), ("pass", 6), ("root",),
        ("L1out",), ("product", 5), ("root",),
        ("gat", 0), ("product", 6), ("pass", 7), ("pass", 8), ("self", 0),
        ("gat", 1), ("product", 7), ("pass", 9), ("pass", 10), ("self", 1),
        ("gat", 2), ("product", 8), ("pass", 11), ("pass", 12), ("self", 2), ("root",),
        ("gate",), ("relate",), ("root",), ("pass", 13), ("root",), ("product", 9), ("product", 10), ("root",)]

_NAMES = ["x", "src", "dst", "edge_type_500", "L0_gnn_W_layer", "L0_gnn_b_layer", "L0_gnn_w_a1", "L0_gnn_b_a1",
          "L0_gnn_w_a2", "L0_gnn_b_a2", "L1_gnn_W_in", "L1_gnn_b_in", "L1_gnn_Ws", "L1_gnn_bs", "L1_gnn_gamma",
          "L1_gnn_beta", "L1_gnn_W_out", "L1_gnn_b_out", "L2_gnn_W1", "L2_gnn_as1", "L2_gnn_ad1", "L2_gnn_b1",
          "L2_gnn_W2", "L2_gnn_as2", "L2_gnn_ad2", "L2_gnn_b2", "L2_gnn_WN", "L2_gnn_asN", "L2_gnn_adN", "L2_gnn_bN",
          "L3_gnn_relation_emb", "L3_gnn_msg_w", "L3_gnn_msg_b", "L3_gnn_upd_w", "L3_gnn_upd_b", "L3_gnn_gate_w",
          "L3_gnn_gate_b"]


def kernel(**inputs):
    import concourse.bacc as bacc
    from concourse.bass_utils import run_bass_kernel_spmd

    nc = bacc.Bacc("TRN2", target_bir_lowering=False, num_devices=1)
    arrays, a = {}, {}
    for name in _NAMES:
        v = np.ascontiguousarray(inputs[name])
        arrays["in_" + name] = v
        a[name] = nc.dram_tensor("in_" + name, v.shape, mybir.dt.from_np(v.dtype), kind="ExternalInput").ap()
    out = nc.dram_tensor("out", (N, D), F32, kind="ExternalOutput").ap()
    row = lambda ap: ap.rearrange("a b -> (a b)")
    mats = {"w_layer": a["L0_gnn_W_layer"], "w_in": a["L1_gnn_W_in"], "ws0": a["L1_gnn_Ws"][0], "ws1": a["L1_gnn_Ws"][1],
            "ws2": a["L1_gnn_Ws"][2], "w_out": a["L1_gnn_W_out"], "w1": a["L2_gnn_W1"], "w2": a["L2_gnn_W2"],
            "wn": a["L2_gnn_WN"]}
    vecs = {"b_layer": a["L0_gnn_b_layer"], "w_a1": row(a["L0_gnn_w_a1"]), "w_a2": row(a["L0_gnn_w_a2"]),
            "b_in": a["L1_gnn_b_in"], "bs0": a["L1_gnn_bs"][0], "bs1": a["L1_gnn_bs"][1], "bs2": a["L1_gnn_bs"][2],
            "gamma": a["L1_gnn_gamma"], "beta": a["L1_gnn_beta"], "b_out": a["L1_gnn_b_out"],
            "as1": row(a["L2_gnn_as1"]), "ad1": row(a["L2_gnn_ad1"]), "b1": a["L2_gnn_b1"],
            "as2": row(a["L2_gnn_as2"]), "ad2": row(a["L2_gnn_ad2"]), "b2": a["L2_gnn_b2"],
            "asn": row(a["L2_gnn_asN"]), "adn": row(a["L2_gnn_adN"]), "bn": a["L2_gnn_bN"],
            "msg_b": row(a["L3_gnn_msg_b"]), "upd_b": row(a["L3_gnn_upd_b"])}
    gnn_program(nc, a["x"], a["src"], a["dst"], a["edge_type_500"], mats, vecs,
                [a["L0_gnn_b_a1"], a["L0_gnn_b_a2"], a["L3_gnn_gate_b"]], a["L3_gnn_relation_emb"],
                row(a["L3_gnn_gate_w"]), {"msg": a["L3_gnn_msg_w"], "upd": a["L3_gnn_upd_w"]}, out)
    r = run_bass_kernel_spmd(nc, [arrays], core_ids=[0])
    return r.results[0]["out"]
```

```python
import numpy as np
from contextlib import ExitStack

import concourse.bass as bass
from concourse import mybir

F32 = mybir.dt.float32
BF16 = mybir.dt.bfloat16
I32 = mybir.dt.int32
ALU = mybir.AluOpType
ACT = mybir.ActivationFunctionType
AX = mybir.AxisListType

P = 128
N = 3125
E = 53125
D = 256
H = 4
R = 500
B = -(-N // P)
LAST = N - (B - 1) * P
EP, EC = 125, 425
U = 8
PU = U // 2
PAIRS = -(-((E + B * (2 * P - 1)) // (2 * P)) // PU) * PU
T = 2 * PAIRS
GROUPS = T // U
TURNS = GROUPS // 2
TX = T + U
W = D + H
NB = 5
DT = B // NB
SC_U = 17
SC_TURNS = EC // SC_U
STAGE_TURNS = (SC_TURNS - SC_TURNS // 2, SC_TURNS // 2)
assert SC_TURNS * SC_U == EC and SC_TURNS % 2 == 1
BANKS = 4
BIG = 2.0 ** 100
LN_EPS = 1e-5
GAT_EPS = 1e-16
SLOPE0, SLOPE2 = 0.01, 0.2
assert EP * EC == E and DT * NB == B and PAIRS * 2 * P > E + B * (2 * P - 1) - 2 * P and GROUPS == 2 * TURNS

CLIFFORD = [[(0, 1), (1, 1), (2, 1), (3, -1)],
            [(1, 1), (0, 1), (3, -1), (2, 1)],
            [(2, 1), (3, 1), (0, 1), (1, -1)],
            [(3, 1), (2, 1), (1, 1), (0, 1)]]

PASSES = [("degree", "src", 1, 0), ("degree", "dst", 1, 0),
          ("max", "src", 1, SLOPE0), ("attend", "src", 1, SLOPE0),
          ("plain", "dst", 1, 0), ("plain", "dst", 1, 0), ("plain", "dst", 1, 0),
          ("max", "dst", H, SLOPE2), ("attend", "dst", H, SLOPE2),
          ("max", "dst", H, SLOPE2), ("attend", "dst", H, SLOPE2),
          ("max", "dst", H, SLOPE2), ("attend", "dst", H, SLOPE2),
          ("relate", "dst", 1, 0)]
PRODUCTS = ["w_layer", "w_in", "ws0", "ws1", "ws2", "w_out", "w1", "w2", "wn", "msg", "upd"]
TURNED = {"w_layer", "msg", "upd"}
VECS = ["b_layer", "w_a1", "w_a2", "b_in", "bs0", "bs1", "bs2", "gamma", "beta", "b_out",
        "as1", "ad1", "b1", "as2", "ad2", "b2", "asn", "adn", "bn", "msg_b", "upd_b"]


def before(n, *kinds):
    return sum(k in kinds for k, _, _, _ in PASSES[:n])


class Order:

    def __init__(self, eng, sem):
        self.eng, self.sem, self.n, self.i, self.per, self.k = eng, sem, 0, None, 0, 0

    def link(self, ins):
        ins.then_inc(self.sem, 1)
        if self.i is None:
            self.n += 1
            self.eng.wait_ge(self.sem, self.n)
        else:
            self.k += 1
            self.eng.wait_ge(self.sem, self.i * self.per + (self.n + self.k))

    def enter(self, i, per):
        self.i, self.per, self.k = i, per, 0

    def leave(self, turns):
        assert self.k == self.per, (self.k, self.per)
        self.n += turns * self.per
        self.i = None


def gnn_program(nc, x, src, dst, etype, mats, vecs, scalars, relation, gate_w, clif_w, out):
    ctx = ExitStack()
    with ctx:
        def sb(name, shape, dt=F32):
            return ctx.enter_context(nc.sbuf_tensor(name, shape, dt))

        def sem(name):
            return ctx.enter_context(nc.semaphore(name))

        table = nc.dram_tensor("node_table", (B * P, D), F32).ap()
        table3 = nc.dram_tensor("node_table_scaled", (B * P, D + 1), F32).ap()
        score_table = nc.dram_tensor("score_table", (B * P, H), F32).ap()
        rel_table = nc.dram_tensor("relation_table", (R, D + 1), F32).ap()
        records = {o: nc.dram_tensor(f"records_{o}", (P * T, 4), I32).ap() for o in ("src", "dst")}

        X = sb("X", [P, B * D])
        HY = sb("HY", [P, 2 * B * D])
        Hh = HY[:, 0:B * D]
        Y = HY[:, B * D:2 * B * D]
        acc = sb("acc", [P, B * W])
        acc3 = acc[:, :].rearrange("p (b w) -> p b w", w=W)
        tmp3 = acc3[:, :, 0:D]
        rec = {o: sb(f"rec_{o}", [P, TX * 4], I32) for o in ("src", "dst")}
        block_of = {o: sb(f"block_of_{o}", [P, PAIRS + PU], I32) for o in ("src", "dst")}
        ES = sb("ES", [P, TX * H])
        G = sb("G", [P, 2 * U, D + 1])
        M = Hh[:, 0:2 * U * W].rearrange("p (u w) -> p u w", w=W)
        OH = sb("OH", [P, 2 * U, P])
        OHT = sb("OHT", [P, U, P])
        NE = OH[:, :, :].rearrange("p u n -> p (u n)").bitcast(BF16)[:, 0:2 * U * P].rearrange("p (u n) -> p u n", n=P)
        XS = OH[:, :, :].rearrange("p u d -> p (u d)")[:, 0:NB * D]
        XT = G[:, :, :].rearrange("p u d -> p (u d)")[:, 0:NB * D]
        wbuf = sb("wbuf", [P, 2, 2, D])
        wraw = sb("wraw", [P, 2, D])
        vec = {n: sb(f"v_{n}", [P, D]) for n in VECS}
        sc = sb("scal", [P, 3])
        ESN = sb("ESN", [P, B * H])
        EDM = sb("EDM", [P, B * 2 * H])
        MX = sb("MX", [P, B * H])
        edge_max = sb("edge_max", [P, H])
        SC = sb("SC", [P, U * H])
        EX = sb("EX", [P, 2, U * H])
        exs = sb("exs", [P, B * H])
        st1 = sb("st1", [P, B])
        st2 = sb("st2", [P, B])
        deg = {o: sb(f"deg_{o}", [P, B]) for o in ("src", "dst")}
        dinv = sb("dinv", [P, B])
        ident = sb("ident", [P, P])
        ones = sb("ones", [P, P])
        before_me = sb("before_me", [P, P])
        iota_n = sb("iota_n", [P, P])
        neg_ident = sb("neg_ident", [P, H, P], BF16)
        iota_i = sb("iota_i", [P, PAIRS], I32)
        gw = sb("gw", [P, D])
        cnt = sb("cnt", [P, B])
        cnt2 = sb("cnt2", [P, B])
        cnt_i = sb("cnt_i", [P, B], I32)
        base = sb("base", [P, B])
        stage = sb("stage", [P, 2, SC_U * 4], I32)
        idx = sb("idx", [P, max(2 * U * 4, 2 * SC_U)], I32)

        A = acc[:, :]
        S_scan = HY[0:EP, 0:B * EC]
        S_src, S_dst, S_typ, S_i, S_adr = (A[0:EP, n * EC:(n + 1) * EC].bitcast(I32) for n in range(5))
        S_q, S_f, S_pos, S_zero = (A[0:EP, (5 + n) * EC:(6 + n) * EC] for n in range(4))
        S_rec = A[0:EP, 9 * EC:13 * EC].bitcast(I32)
        S_recf = A[0:EP, 9 * EC:13 * EC]
        assert 13 * EC <= B * W
        fill = G[:, :, :].rearrange("p u d -> p (u d)")[:, 0:T * 4]
        assert T * 4 <= 2 * U * (D + 1) and 2 * PAIRS <= U * P
        iota_t = OHT[:, :, :].rearrange("p u d -> p (u d)")[:, 0:PAIRS]
        bt_f = OHT[:, :, :].rearrange("p u d -> p (u d)")[:, PAIRS:2 * PAIRS]

        ps = ctx.enter_context(nc.psum_tensor("ps", [P, 8, 512], F32))
        psf = ps[:, :, :].rearrange("p b n -> p (b n)")
        T_ps = psf[:, 4 * 512:6 * 512]
        EDM_ps = ps[:, 6, 0:U * 2 * H]
        XT_ps = psf[:, 0:NB * D]
        Y_ps = psf[:, 3 * 512:3 * 512 + NB * D]

        s_load, s_const, s_order, s_gorder, s_aorder = sem("loaded"), sem("constants"), sem("dve_order"), sem("pool_order"), sem("act_order")
        s_cnt, s_offs, s_fill, s_filled, s_adr = (sem(n) for n in (
            "counts_ready", "offsets_ready", "fill_ready", "filled", "addresses_ready"))
        s_in, s_xs, s_xt_ps, s_xt, s_y_ps, s_y = (sem(n) for n in (
            "product_input", "xs_ready", "xt_in_psum", "xt_ready", "y_in_psum", "y_ready"))
        s_wraw, s_wT_ps, s_wT, s_kneg, s_kraw = (sem(n) for n in (
            "raw_weight_loaded", "weight_turned", "weight_ready", "clifford_signed", "clifford_loaded"))
        s_w = [sem(f"weight_loaded{k}") for k in range(2)]
        s_sorted = [sem(f"sorted{k}") for k in range(2)]
        s_rec = {o: sem(f"records_loaded_{o}") for o in ("src", "dst")}
        s_idx = sem("indices_ready")
        s_sq_in, s_sq = sem("root_input"), sem("root_ready")
        s_hfree, s_relld = sem("h_free"), sem("relation_loaded")
        landed = [sem(f"landed{k}") for k in range(2 * U)]
        rel_landed = [sem(f"rel_landed{k}") for k in range(2 * U)]
        s_oh, s_ps, s_psfree, s_msg = (sem(n) for n in (
            "onehot_ready", "sum_in_psum", "psum_free", "message_ready"))
        s_T, s_OHT, s_edm, s_sc, s_ex = (sem(n) for n in (
            "turned_in_psum", "turned_ready", "target_scores_ready", "scores_ready", "exp_ready"))
        s_tab_sc, s_tab, s_stab_st, s_tab_st = (sem(n) for n in (
            "score_table_ready", "table_ready", "score_table_stored", "table_stored"))
        s_self, s_selfx, s_rel, s_relst, s_gz, s_gs, s_out, s_fin = (sem(n) for n in (
            "self_scores_ready", "self_exp_ready", "relation_rows_ready", "relation_stored",
            "gate_sum_ready", "gate_ready", "output_ready", "stored"))

        tab_view = table.rearrange("(b p) d -> p b d", p=P)
        tab3_view = table3.rearrange("(b p) d -> p b d", p=P)
        stab_view = score_table.rearrange("(b p) d -> p b d", p=P)
        Y3 = Y.rearrange("p (b d) -> p b d", d=D)
        H3 = Hh.rearrange("p (b d) -> p b d", d=D)
        X3 = X[:, :].rearrange("p (b d) -> p b d", d=D)
        scaled3 = acc[:, 0:B * (D + 1)].rearrange("p (b d) -> p b d", d=D + 1)
        R4 = Hh[0:EP, 0:4 * (D + 1)].rearrange("p (q d) -> p q d", d=D + 1)
        R4t = Y[0:EP, 0:4 * D].rearrange("p (q d) -> p q d", d=D)

        def load_blocks(eng, o, at):
            _, regs = nc.values_load_multi_w_load_instructions(
                block_of[o][0:1, bass.ds(at, PU)], engines=(eng.engine,), min_val=0, max_val=B - 1,
                skip_runtime_bounds_check_because="a block number counts at most B - 1 comparisons")
            return regs

        RAW_LOADS = 3 + 2 + len(VECS) + 3 + 1
        block = ctx.enter_context(nc.Block())

        @block.sync
        def _(sp):
            sp.dma_start(S_src, src.rearrange("(p c) -> p c", c=EC)).then_inc(s_load, 16)
            sp.dma_start(S_dst, dst.rearrange("(p c) -> p c", c=EC)).then_inc(s_load, 16)
            sp.dma_start(S_typ, etype.rearrange("(p c) -> p c", c=EC)).then_inc(s_load, 16)
            sp.wait_ge(s_const, 1)
            sp.dma_start(X3[:, 0:B - 1, :], x[0:(B - 1) * P, :].rearrange("(b p) d -> p b d", p=P)).then_inc(s_load, 16)
            sp.dma_start(X3[0:LAST, B - 1, :], x[(B - 1) * P:N, :]).then_inc(s_load, 16)
            for n in VECS:
                sp.dma_start(vec[n][:, :], vecs[n].partition_broadcast(P)).then_inc(s_load, 16)
            for n in range(3):
                sp.dma_start(sc[:, n:n + 1], scalars[n].partition_broadcast(P)).then_inc(s_load, 16)
            sp.dma_start(gw[:, :], gate_w.partition_broadcast(P)).then_inc(s_load, 16)
            sp.wait_ge(s_fill, 1)
            for o in ("src", "dst"):
                sp.dma_start(records[o].rearrange("(p t) f -> p (t f)", p=P), fill.bitcast(I32)).then_inc(s_filled, 16)
            for n, o in enumerate(("src", "dst")):
                for s_, turns in zip(s_sorted, STAGE_TURNS):
                    sp.wait_ge(s_, 16 * SC_U * turns * (n + 1))
                sp.dma_start(rec[o][:, 0:T * 4], records[o].rearrange("(p t) f -> p (t f)", p=P)).then_inc(s_rec[o], 16)

            def load_weight(j):
                name = PRODUCTS[j]
                if j >= 2:
                    sp.wait_ge(s_y_ps, 1 + DT * (j - 1))
                if name in ("msg", "upd"):
                    sp.wait_ge(s_wT_ps, 1 if name == "msg" else 2)
                    for i in range(4):
                        for jj, (w, _) in enumerate(CLIFFORD[i]):
                            sp.dma_start(wraw[64 * (i % 2):64 * (i % 2) + 64, i // 2, 64 * jj:64 * jj + 64],
                                         clif_w[name][w, :, :]).then_inc(s_kraw, 16)
                elif name in TURNED:
                    sp.dma_start(wraw[:, :, :], mats[name].rearrange("(k p) n -> p k n", p=P)).then_inc(s_wraw, 16)
                else:
                    sp.dma_start(wbuf[:, j % 2, :, :], mats[name].rearrange("(k p) n -> p k n", p=P)).then_inc(s_w[j % 2], 16)

            def store_tables(stage):
                sp.wait_ge(s_tab_sc, stage)
                sp.dma_start(stab_view, ESN[:, :].rearrange("p (b h) -> p b h", h=H)).then_inc(s_stab_st, 16)

            load_weight(0)
            load_weight(1)
            score_stage = 0
            for n in range(7):
                j = (0, 2, 3, 4, 6, 7, 8)[n]
                if n == 0 or n >= 4:
                    score_stage += 1
                    store_tables(score_stage)
                sp.wait_ge(s_tab, n + 1)
                sp.dma_start(tab_view, Y3).then_inc(s_tab_st, 16)
                for jj in {0: (2,), 1: (3,), 2: (4,), 3: (5, 6), 4: (7,), 5: (8,), 6: (9,)}[n]:
                    load_weight(jj)
            sp.wait_ge(s_hfree, 1)
            sp.dma_start(R4[:, :, 0:D], relation.rearrange("(q p) d -> p q d", p=EP)).then_inc(s_relld, 16)
            sp.wait_ge(s_rel, 1)
            sp.dma_start(rel_table.rearrange("(q p) d -> p q d", p=EP), R4).then_inc(s_relst, 16)
            sp.wait_ge(s_tab, 8)
            sp.dma_start(tab3_view, scaled3).then_inc(s_tab_st, 16)
            load_weight(10)
            sp.wait_ge(s_out, 1)
            sp.dma_start(out[0:(B - 1) * P, :].rearrange("(b p) d -> p b d", p=P), X3[:, 0:B - 1, :]).then_inc(s_fin, 16)
            sp.dma_start(out[(B - 1) * P:N, :], X3[0:LAST, B - 1, :]).then_inc(s_fin, 16)
            sp.wait_ge(s_fin, 32)

        @block.gpsimd
        def _(pool):
            order = Order(pool, s_gorder)
            pool.memset(X3[:, B - 1, :], 0.0).then_inc(s_const, 1)
            order.link(pool.memset(ident[:, :], 0.0))
            order.link(pool.affine_select(out=ident[:, :], in_=ident[:, :], compare_op=ALU.not_equal, fill=1.0,
                                          base=0, pattern=[[-1, P]], channel_multiplier=1))
            order.link(pool.memset(ones[:, :], 1.0))
            order.link(pool.affine_select(out=before_me[:, :], in_=ones[:, :], compare_op=ALU.is_gt, fill=0.0,
                                          base=0, pattern=[[1, P]], channel_multiplier=-1))
            pool.iota(iota_i[:, :], pattern=[[1, PAIRS]], base=0, channel_multiplier=0).then_inc(s_const, 1)

            pool.wait_ge(s_filled, 32)
            for n, o in enumerate(("src", "dst")):
                pool.wait_ge(s_adr, n + 1)

                def turn(t, st, past):
                    served = STAGE_TURNS[st] * n + past
                    if not (isinstance(served, int) and served == 0):
                        pool.wait_ge(s_sorted[st], served * (16 * SC_U))
                    pool.tensor_copy(idx[0:EP, st * SC_U:(st + 1) * SC_U], S_adr[:, bass.ds(t * SC_U, SC_U)]).then_inc(s_idx, 1)
                    pool.tensor_copy(stage[0:EP, st, :], S_rec[:, bass.ds(t * (SC_U * 4), SC_U * 4)]).then_inc(s_idx, 1)
                    pool.wait_ge(s_idx, t * 2 + (2 * n * SC_TURNS + 2))
                    pool.nop(nofuse=True)
                    for k in range(SC_U):
                        pool.indirect_dma_start(
                            out=records[o][:, :],
                            out_offset=bass.IndirectOffsetOnAxis(ap=idx[0:EP, st * SC_U + k:st * SC_U + k + 1], axis=0),
                            in_=stage[0:EP, st, 4 * k:4 * k + 4], in_offset=None).then_inc(s_sorted[st], 16)

                turn(0, 0, 0)
                turn(1, 1, 0)
                turn(2, 0, 1)
                with pool.Fori(0, (SC_TURNS - 3) // 2) as i:
                    turn(i * 2 + 3, 1, i + 1)
                    turn(i * 2 + 4, 0, i + 2)

            def gather(n, dest, tab, col, sems, use):
                o = PASSES[n][1]
                with pool.Fori(0, TURNS) as i:
                    for g in range(2):
                        pool.wait_ge(s_psfree, i * (2 * PU) + (BANKS + n * PAIRS + (g - 1) * PU))
                        pool.tensor_copy(idx[:, g * U * 4:(g + 1) * U * 4],
                                         rec[o][:, bass.ds((i * 2 + g) * (U * 4), U * 4)]).then_inc(s_idx, 1)
                        pool.wait_ge(s_idx, i * 2 + (4 * SC_TURNS + use * GROUPS + g + 1))
                        pool.nop(nofuse=True)
                        for k in range(g * U, (g + 1) * U):
                            for d_, t_, c_, s_ in zip(dest, tab, col, sems):
                                pool.indirect_dma_start(
                                    out=d_(k), out_offset=None, in_=t_,
                                    in_offset=bass.IndirectOffsetOnAxis(
                                        ap=idx[:, k * 4 + c_:k * 4 + c_ + 1], axis=0)).then_inc(s_[k], 16)

            for o in ("src", "dst"):
                pool.wait_ge(s_rec[o], 16)
            tables = scores = 0
            for n, (kind, o, heads, _) in enumerate(PASSES):
                use = before(n, "max", "attend", "plain", "relate")
                if kind == "max":
                    scores += 1
                    pool.wait_ge(s_stab_st, 16 * scores)
                    gather(n, [lambda k: G[:, k, 0:H]], [score_table[:, :]], [0], [landed], use)
                elif kind in ("attend", "plain"):
                    tables += 1
                    pool.wait_ge(s_tab_st, 16 * tables)
                    gather(n, [lambda k: G[:, k, 0:D]], [table[:, :]], [0], [landed], use)
                elif kind == "relate":
                    pool.wait_ge(s_tab_st, 16 * (tables + 1))
                    pool.wait_ge(s_relst, 16)
                    gather(n, [lambda k: G[:, k, :], lambda k: M[:, k, 0:D + 1]], [table3[:, :], rel_table[:, :]],
                           [0, 2], [landed, rel_landed], use)

        @block.tensor
        def _(pe):
            def offsets(n):
                pe.wait_ge(s_const, 2)
                pe.wait_ge(s_cnt, n + 1)
                nc.tensor.matmul(ps[0:EP, 0, 0:B], before_me[0:EP, 0:EP], cnt[0:EP, :], start=True, stop=True)
                nc.tensor.matmul(ps[:, 1, 0:B], ones[0:EP, :], cnt[0:EP, :], start=True, stop=True).then_inc(s_offs, 1)

            turned = [0]

            def turn_weight(j):
                name = PRODUCTS[j]
                if name not in TURNED:
                    return
                if name == "w_layer":
                    pe.wait_ge(s_wraw, 16)
                else:
                    pe.wait_ge(s_kneg, turned[0])
                for k in range(2):
                    for m in range(2):
                        last = nc.tensor.transpose(ps[:, 6 + k, m * P:(m + 1) * P], wraw[:, m, k * P:(k + 1) * P], ident[:, :])
                last.then_inc(s_wT_ps, 1)
                turned[0] += 1

            loaded = [0, 0]

            def product(j):
                turn_weight(j)
                if PRODUCTS[j] in TURNED:
                    pe.wait_ge(s_wT, turned[0])
                else:
                    loaded[j % 2] += 1
                    pe.wait_ge(s_w[j % 2], 16 * loaded[j % 2])
                with pe.Fori(0, DT) as i:
                    pe.wait_ge(s_xs, i + (DT * j + 1))
                    for q in range(2 * NB):
                        last = nc.tensor.transpose(XT_ps[:, q * P:(q + 1) * P], XS[:, q * P:(q + 1) * P], ident[:, :])
                    last.then_inc(s_xt_ps, 1)
                    pe.wait_ge(s_xt, i + (DT * j + 1))
                    pe.wait_ge(s_y, i + (1 + DT * j))
                    for q in range(NB):
                        for k in range(2):
                            last = nc.tensor.matmul(Y_ps[:, q * D:(q + 1) * D], XT[:, (2 * q + k) * P:(2 * q + k + 1) * P],
                                                    wbuf[:, j % 2, k, :], start=(k == 0), stop=(k == 1))
                    last.then_inc(s_y_ps, 1)

            def tile_pass(n):
                kind, o, heads, _ = PASSES[n]
                use = before(n, "max", "attend", "plain", "relate")
                att, msg = before(n, "attend"), before(n, "attend", "relate")

                def look_ahead(i, ahead, g):
                    pe.wait_ge(s_oh, i * 2 + (n * (GROUPS + 1) + ahead + 1))
                    if kind != "attend":
                        return
                    if ahead:
                        pe.wait_ge(s_sc, i * 2 + (att * (GROUPS + 1) + ahead))
                    for k in range(U):
                        last = nc.tensor.transpose(T_ps[:, k * P:(k + 1) * P], OH[:, g * U + k, :], ident[:, :])
                    last.then_inc(s_T, 1)
                    pe.wait_ge(s_OHT, i * 2 + (att * (GROUPS + 1) + ahead + 1))
                    blocks = load_blocks(pe, o, (i * 2 + ahead) * PU)
                    for k in range(U):
                        last = nc.tensor.matmul(EDM_ps[:, k * 2 * H:(k + 1) * 2 * H], OHT[:, k, :],
                                                EDM[:, bass.ds(blocks[k // 2] * (2 * H), 2 * H)], start=True, stop=True)
                    last.then_inc(s_edm, 1)

                def sums(i, g, pairs):
                    for q in pairs:
                        pe.wait_ge(s_psfree, i * (2 * PU) + (n * PAIRS + g * PU + q + 1))
                        for k in (2 * q, 2 * q + 1):
                            s = g * U + k
                            first, end = k == 2 * q, k == 2 * q + 1
                            if kind == "degree":
                                last = nc.tensor.matmul(ps[:, q, 0:1], OH[:, s, :], ones[:, 0:1], start=first, stop=end)
                            elif kind == "max":
                                pe.wait_ge(landed[s], i * 16 + 16 * (use * TURNS + 1))
                                nc.tensor.matmul(ps[:, k, 0:heads * P], NE[:, s, :],
                                                 neg_ident[:, 0:heads, :], start=True, stop=False)
                                for h in range(heads):
                                    last = nc.tensor.matmul(ps[:, k, h * P:(h + 1) * P], G[:, s, h:h + 1].to_broadcast([P, P]),
                                                            ident[:, :], start=False, stop=(h == heads - 1))
                            elif kind == "plain":
                                pe.wait_ge(landed[s], i * 16 + 16 * (use * TURNS + 1))
                                last = nc.tensor.matmul(ps[:, q, 0:D], OH[:, s, :], G[:, s, 0:D], start=first, stop=end)
                            else:
                                pe.wait_ge(s_msg, i * (2 * U) + (msg * T + s + 1))
                                w = W if heads == H else D + 1
                                last = nc.tensor.matmul(ps[:, q, 0:w], OH[:, s, :], M[:, s, 0:w], start=first, stop=end)
                        last.then_inc(s_ps, 1)

                look_ahead(0, 0, 0)
                with pe.Fori(0, TURNS) as i:
                    for g in range(2):
                        sums(i, g, range(PU // 2))
                        look_ahead(i, g + 1, 1 - g)
                        sums(i, g, range(PU // 2, PU))

            offsets(0)
            offsets(1)
            for step in PLAN:
                product(step[1]) if step[0] == "product" else tile_pass(step[1]) if step[0] == "pass" else None

        @block.scalar
        def _(act):
            turned = [0]

            def product(j):
                name = PRODUCTS[j]
                if name in TURNED:
                    if name != "w_layer":
                        act.wait_ge(s_kraw, 16 * 16 * turned[0])
                        negs = [(i, jj) for i in range(4) for jj in range(4) if CLIFFORD[i][jj][1] < 0]
                        for i, jj in negs:
                            w = wraw[64 * (i % 2):64 * (i % 2) + 64, i // 2, 64 * jj:64 * jj + 64]
                            last = nc.scalar.mul(w, w, -1.0)
                        last.then_inc(s_kneg, 1)
                    turned[0] += 1
                    act.wait_ge(s_wT_ps, turned[0])
                    nc.scalar.copy(wbuf[:, j % 2, :, :], ps[:, 6:8, 0:D]).then_inc(s_wT, 1)
                act.wait_ge(s_in, j + 1)
                source = X if name in ("w_layer", "w_in", "w1") else HY
                with act.Fori(0, DT) as i:
                    act.wait_ge(s_xt_ps, i + (1 + DT * j))
                    nc.scalar.copy(XS, source[:, bass.ds(i * (NB * D), NB * D)]).then_inc(s_xs, 1)
                    act.wait_ge(s_xt_ps, i + (1 + DT * j + 1))
                    act.wait_ge(s_y_ps, i + (1 + DT * j))
                    nc.scalar.copy(XT, XT_ps).then_inc(s_xt, 1)

            def tile_pass(n):
                if PASSES[n][0] != "attend":
                    return
                att = before(n, "attend")

                def look_ahead(i, ahead, g):
                    act.wait_ge(s_T, i * 2 + (att * (GROUPS + 1) + ahead + 1))
                    if ahead:
                        act.wait_ge(s_edm, i * 2 + (att * (GROUPS + 1) + ahead))
                    nc.scalar.copy(OHT[:, :, :].rearrange("p u n -> p (u n)"), T_ps).then_inc(s_OHT, 1)
                    act.wait_ge(s_sc, i * 2 + (att * (GROUPS + 1) + ahead + 1))
                    if ahead:
                        act.wait_ge(s_msg, i * (2 * U) + (before(n, "attend", "relate") * T + (ahead - 1) * U))
                    nc.scalar.activation(EX[:, g, :], SC[:, :], ACT.Exp).then_inc(s_ex, 1)

                look_ahead(0, 0, 0)
                with act.Fori(0, TURNS) as i:
                    for g in range(2):
                        look_ahead(i, g + 1, 1 - g)

            n_self = roots = 0
            for step in PLAN:
                if step[0] == "product":
                    product(step[1])
                elif step[0] == "pass":
                    tile_pass(step[1])
                elif step[0] == "self":
                    n_self += 1
                    act.wait_ge(s_self, n_self)
                    nc.scalar.activation(exs[:, :], exs[:, :], ACT.Exp).then_inc(s_selfx, 1)
                elif step[0] == "root":
                    roots += 1
                    act.wait_ge(s_sq_in, roots)
                    nc.scalar.activation(st2[:, :], st2[:, :], ACT.Sqrt).then_inc(s_sq, 1)
                elif step[0] == "gate":
                    act.wait_ge(s_gz, 1)
                    nc.scalar.activation(cnt[0:EP, 0:4], cnt[0:EP, 0:4], ACT.Exp, scale=-1.0).then_inc(s_gs, 1)

        @block.vector
        def _(dve):
            order = Order(dve, s_order)
            L = order.link
            v = nc.vector
            nb = lambda ap, w=D: ap.unsqueeze(2).to_broadcast([P, B, w])
            vb = lambda ap: ap.unsqueeze(1).to_broadcast([P, B, D])

            def sort(n, o):
                key, other = (S_src, S_dst) if o == "src" else (S_dst, S_src)
                if n:
                    for s_, turns in zip(s_sorted, STAGE_TURNS):
                        dve.wait_ge(s_, 16 * SC_U * turns * n)
                L(v.tensor_scalar(S_i, key, 7, None, ALU.logical_shift_right))
                L(v.tensor_copy(S_q, S_i))
                L(v.tensor_scalar(S_i, key, P - 1, None, ALU.bitwise_and))
                r = S_rec.rearrange("p (c f) -> p c f", f=4)
                v.tensor_copy(S_recf.rearrange("p (c f) -> p c f", f=4)[:, :, 1:2], S_i.unsqueeze(2))
                v.tensor_copy(r[:, :, 0:1], other.unsqueeze(2))
                v.tensor_copy(r[:, :, 2:3], S_typ.unsqueeze(2))
                v.memset(r[:, :, 3:4], 0)
                L(v.memset(S_zero, 0.0))
                with dve.Fori(0, B) as b:
                    order.enter(b, 2)
                    L(v.tensor_scalar(S_f, S_q, iota_n[0:EP, bass.ds(b, 1)], None, ALU.is_equal))
                    L(v.tensor_tensor_scan(S_scan[:, bass.ds(b * EC, EC)], S_f, S_zero, 0.0, ALU.add, ALU.add))
                    order.leave(B)
                scan3 = S_scan.rearrange("p (b c) -> p b c", c=EC)
                v.tensor_copy(cnt[0:EP, :].unsqueeze(2), scan3[:, :, EC - 1:EC]).then_inc(s_cnt, 1)
                dve.wait_ge(s_offs, n + 1)
                L(v.tensor_scalar(cnt_i[:, :], ps[:, 1, 0:B], float(2 * P - 1), None, ALU.add))
                L(v.tensor_scalar(cnt_i[:, :], cnt_i[:, :], 8, None, ALU.logical_shift_right))
                L(v.tensor_copy(cnt2[:, :], cnt_i[:, :]))
                L(v.tensor_tensor_scan(base[:, :], cnt2[:, :], nul_b, 0.0, ALU.add, ALU.add))
                L(v.tensor_tensor(cnt2[:, :], base[:, :], cnt2[:, :], ALU.subtract))
                L(v.scalar_tensor_tensor(base[0:EP, :], cnt2[0:EP, :], float(2 * P), ps[0:EP, 0, 0:B], ALU.mult, ALU.add))
                L(v.tensor_scalar(base[0:EP, :], base[0:EP, :], -1.0, None, ALU.add))
                L(v.tensor_tensor(scan3, scan3, base[0:EP, :].unsqueeze(2).to_broadcast([EP, B, EC]), ALU.add))
                L(v.memset(S_pos, 0.0))
                with dve.Fori(0, B) as b:
                    order.enter(b, 2)
                    L(v.scalar_tensor_tensor(S_f, S_q, iota_n[0:EP, bass.ds(b, 1)], S_scan[:, bass.ds(b * EC, EC)],
                                             ALU.is_equal, ALU.mult))
                    L(v.tensor_tensor(S_pos, S_pos, S_f, ALU.add))
                    order.leave(B)
                L(v.tensor_copy(S_adr, S_pos))
                L(v.tensor_scalar(S_i, S_adr, P - 1, None, ALU.bitwise_and))
                L(v.tensor_scalar(S_adr, S_adr, 7, None, ALU.logical_shift_right))
                L(v.tensor_copy(S_f, S_i))
                L(v.tensor_copy(S_pos, S_adr))
                L(v.scalar_tensor_tensor(S_f, S_f, float(T), S_pos, ALU.mult, ALU.add))
                v.tensor_copy(S_adr, S_f).then_inc(s_adr, 1)
                L(v.memset(bt_f, 0.0))
                with dve.Fori(0, B - 1) as b:
                    order.enter(b, 1)
                    L(v.scalar_tensor_tensor(bt_f, iota_t, cnt2[:, bass.ds(b + 1, 1)], bt_f, ALU.is_ge, ALU.add))
                    order.leave(B - 1)
                L(v.tensor_copy(block_of[o][:, 0:PAIRS], bt_f))

            def product(j, finish):
                with dve.Fori(0, DT) as i:
                    dve.wait_ge(s_y_ps, i + (1 + DT * j + 1))
                    finish(Y if j != 1 else Hh, i).then_inc(s_y, 1)
                dve.wait_ge(s_y, 1 + DT * (j + 1))

            def add_bias(name):
                def f(where, i):
                    return v.tensor_tensor(where[:, bass.ds(i * (NB * D), NB * D)].rearrange("p (b d) -> p b d", d=D),
                                           Y_ps.rearrange("p (b d) -> p b d", d=D),
                                           vec[name][:, :].unsqueeze(1).to_broadcast([P, NB, D]), ALU.add)
                return f

            def scaled(where, i):
                return v.tensor_tensor(where[:, bass.ds(i * (NB * D), NB * D)].rearrange("p (b d) -> p b d", d=D),
                                       Y_ps.rearrange("p (b d) -> p b d", d=D),
                                       dinv[:, bass.ds(i * NB, NB)].unsqueeze(2).to_broadcast([P, NB, D]), ALU.mult)

            def copied(where, i):
                return v.tensor_copy(where[:, bass.ds(i * (NB * D), NB * D)], Y_ps)

            def tile_pass(n):
                kind, o, heads, slope = PASSES[n]
                use = before(n, "max", "attend", "plain", "relate")
                att = before(n, "attend")
                where = {"degree": (deg[o], 1, 1), "max": (MX, H, heads), "plain": (acc, W, D)}.get(
                    kind, (acc, W, W if heads == H else D + 1))
                dloc = rec[o][:, :].bitcast(F32)
                links = 2 * {"degree": 0, "max": PU, "plain": 0, "relate": 0, "attend": 3}[kind]

                def one_hot(i, ahead, g):
                    local = dloc[:, bass.ds((i * 2 + ahead) * (U * 4), U * 4)].rearrange("p (u f) -> p u f", f=4)[:, :, 1:2]
                    v.tensor_tensor((NE if kind == "max" else OH)[:, g * U:(g + 1) * U, :],
                                    iota_n[:, :].unsqueeze(1).to_broadcast([P, U, P]), local.to_broadcast([P, U, P]),
                                    ALU.not_equal if kind == "max" else ALU.is_equal).then_inc(s_oh, 1)

                def edge_scores(i, ahead, g):
                    dve.wait_ge(s_edm, i * 2 + (att * (GROUPS + 1) + ahead + 1))
                    if ahead:
                        dve.wait_ge(s_ex, i * 2 + (att * (GROUPS + 1) + ahead))
                    edm = EDM_ps.rearrange("p (u s h) -> p u s h", u=U, h=H)
                    s3 = SC[:, :].rearrange("p (u h) -> p u h", h=H)
                    L(v.tensor_tensor(s3, ES[:, bass.ds((i * 2 + ahead) * (U * H), U * H)].rearrange("p (u h) -> p u h", h=H),
                                      edm[:, :, 0, :], ALU.add))
                    L(v.scalar_tensor_tensor(SC[:, :], SC[:, :], slope, SC[:, :], ALU.mult, ALU.max))
                    L(v.tensor_tensor(s3, s3, edm[:, :, 1, :], ALU.subtract))
                    v.tensor_scalar(SC[:, :], SC[:, :], 0.0, None, ALU.min).then_inc(s_sc, 1)

                def message(i, g, k):
                    s = g * U + k
                    dve.wait_ge(landed[s], i * 16 + 16 * (use * TURNS + 1))
                    if kind == "relate":
                        dve.wait_ge(rel_landed[s], i * 16 + 16)
                        ins = v.tensor_tensor(M[:, s, 0:D + 1], M[:, s, 0:D + 1], G[:, s, :], ALU.mult)
                    elif heads == 1:
                        ins = v.tensor_scalar(M[:, s, 0:D], G[:, s, 0:D], EX[:, g, k * H:k * H + 1], None, ALU.mult)
                    else:
                        ins = v.tensor_tensor(M[:, s, 0:D].rearrange("p (h c) -> p h c", h=H),
                                              G[:, s, 0:D].rearrange("p (h c) -> p h c", h=H),
                                              EX[:, g, k * H:(k + 1) * H].unsqueeze(2).to_broadcast([P, H, D // H]), ALU.mult)
                    ins.then_inc(s_msg, 1)

                def drain(i, g, q, blocks):
                    dve.wait_ge(s_ps, i * (2 * PU) + (n * PAIRS + g * PU + q + 1))
                    full, stride, w = where
                    part = full[:, bass.ds(blocks[q] * stride, w)]
                    dve.wait_ge(s_psfree, i * (2 * PU) + (BANKS + n * PAIRS + g * PU + q))
                    if kind == "max":
                        if q == PU - 1:
                            v.tensor_copy(ES[:, bass.ds((i * 2 + g) * (U * H), U * H)].rearrange("p (u h) -> p u h", h=H),
                                          G[:, g * U:(g + 1) * U, 0:H])
                        L(v.tensor_reduce(edge_max[:, 0:heads],
                                          ps[:, 2 * q:2 * q + 2, 0:heads * P].rearrange("p t (h e) -> p h t e", h=heads),
                                          AX.XY, ALU.max))
                    if kind == "max":
                        ins = v.tensor_tensor(part, part, edge_max[:, 0:heads], ALU.max)
                    else:
                        ins = v.tensor_tensor(part, part, ps[:, q, 0:w], ALU.add)
                    ins.then_inc(s_psfree, 1)

                one_hot(0, 0, 0)
                if kind == "attend":
                    edge_scores(0, 0, 0)
                with dve.Fori(0, TURNS) as i:
                    order.enter(i, links)
                    for g in range(2):
                        blocks = load_blocks(dve, o, (i * 2 + g) * PU)
                        one_hot(i, g + 1, 1 - g)
                        if kind in ("attend", "relate"):
                            if kind == "attend":
                                dve.wait_ge(s_ex, i * 2 + (att * (GROUPS + 1) + g + 1))
                                v.tensor_copy(M[:, g * U:(g + 1) * U, D:D + H],
                                              EX[:, g, :].rearrange("p (u h) -> p u h", h=H))
                            for k in range(U):
                                message(i, g, k)
                                if k % 2 and k > 1:
                                    drain(i, g, k // 2 - 1, blocks)
                                if k == U - 3 and kind == "attend":
                                    edge_scores(i, g + 1, 1 - g)
                            drain(i, g, PU - 1, blocks)
                        else:
                            for q in range(PU):
                                drain(i, g, q, blocks)
                    order.leave(TURNS)
                L(v.memset(st1[:, :], 0.0))

            roots = [0]

            def inverse_root(dest):
                roots[0] += 1
                dve.wait_ge(s_sq, roots[0])
                L(v.reciprocal(dest[:, :], st2[:, :]))

            def layer_norm(a3, tmp, gamma=None, beta=None):
                L(v.tensor_reduce(st1[:, :], a3, AX.X, ALU.add))
                L(v.tensor_scalar(st1[:, :], st1[:, :], 1.0 / D, None, ALU.mult))
                L(v.tensor_tensor(a3, a3, nb(st1[:, :]), ALU.subtract))
                L(v.tensor_tensor(tmp, a3, a3, ALU.mult))
                L(v.tensor_reduce(st2[:, :], tmp, AX.X, ALU.add))
                v.tensor_scalar(st2[:, :], st2[:, :], 1.0 / D, LN_EPS, ALU.mult, ALU.add).then_inc(s_sq_in, 1)
                inverse_root(st2)
                L(v.tensor_tensor(a3, a3, nb(st2[:, :]), ALU.mult))
                if gamma is not None:
                    L(v.tensor_tensor(a3, a3, vb(gamma), ALU.mult))
                    L(v.tensor_tensor(a3, a3, vb(beta), ALU.add))

            EDM4 = EDM[:, :].rearrange("p (b s h) -> p b s h", s=2, h=H)
            ESN3 = ESN[:, :].rearrange("p (b h) -> p b h", h=H)
            MX3 = MX[:, :].rearrange("p (b h) -> p b h", h=H)
            exs3 = exs[:, :].rearrange("p (b h) -> p b h", h=H)

            def score(dest, a, heads):
                L(v.tensor_tensor(tmp3, Y3, vb(a), ALU.mult))
                c = D // heads
                for h in range(heads):
                    L(v.tensor_reduce(dest(h), tmp3[:, :, h * c:(h + 1) * c], AX.X, ALU.add))

            def maxima(slope):
                m = EDM4[:, :, 1, :]
                L(v.tensor_tensor(m, MX3, EDM4[:, :, 0, :], ALU.add))
                L(v.scalar_tensor_tensor(m, m, slope, m, ALU.mult, ALU.max))

            nul_b = exs[:, 0:B]
            dve.wait_ge(s_const, 2)
            v.memset(exs[:, :], 0.0)
            v.memset(ESN[:, :], 0.0)
            v.memset(EDM[:, :], 0.0)
            v.memset(edge_max[:, :], 0.0)
            v.memset(deg["src"][:, :], 0.0)
            v.memset(deg["dst"][:, :], 0.0)
            v.tensor_copy(iota_n[:, :], iota_i[:, 0:P])
            v.tensor_copy(iota_t, iota_i[:, 0:PAIRS])
            v.memset(ES[:, T * H:TX * H], 0.0)
            for o in ("src", "dst"):
                v.memset(rec[o][:, T * 4:TX * 4].bitcast(F32), -1.0)
                v.memset(block_of[o][:, PAIRS:PAIRS + PU], 0)
            L(v.memset(fill, 0.0))
            v.memset(fill.rearrange("p (t f) -> p t f", f=4)[:, :, 1:2], -1.0).then_inc(s_fill, 1)
            dve.sem_inc(s_psfree, BANKS)
            for s in (s_y, s_y_ps, s_xt_ps):
                dve.sem_inc(s, 1)
            dve.wait_ge(s_load, 16 * RAW_LOADS)
            for h in range(H):
                L(v.tensor_scalar(neg_ident[:, h, :], ident[:, :], -BIG, None, ALU.mult))
            sort(0, "src")
            sort(1, "dst")
            tables = [0]

            def table_ready(ins):
                ins.then_inc(s_tab, 1)

            def attention(scale_first, n_max, n_att, heads, slope, src_vec, dst_vec, self_loop):
                score(lambda h: ESN3[:, :, h:h + 1], vec[src_vec][:, :], heads)
                if not self_loop:
                    L(v.tensor_scalar(ESN3[:, :, 0:1], ESN3[:, :, 0:1], sc[:, 1:2], None, ALU.add))
                v.tensor_copy(exs[:, :], ESN[:, :]).then_inc(s_tab_sc, 1)
                score(lambda h: EDM4[:, :, 0, h:h + 1], vec[dst_vec][:, :], heads)
                if not self_loop:
                    L(v.tensor_scalar(EDM4[:, :, 0, 0:1], EDM4[:, :, 0, 0:1], sc[:, 0:1], None, ALU.add))
                if self_loop:
                    L(v.tensor_copy(MX[:, :], ESN[:, :]))
                else:
                    L(v.memset(MX[:, :], -BIG))
                tile_pass(n_max)
                maxima(slope)
                L(v.memset(acc[:, :], 0.0))
                tile_pass(n_att)
                if self_loop:
                    L(v.tensor_tensor(exs3, ESN3, EDM4[:, :, 0, :], ALU.add))
                    L(v.scalar_tensor_tensor(exs[:, :], exs[:, :], slope, exs[:, :], ALU.mult, ALU.max))
                    v.tensor_tensor(exs3, exs3, EDM4[:, :, 1, :], ALU.subtract).then_inc(s_self, 1)

            n_self = 0
            n_tab = 0
            for step in PLAN:
                what = step[0]
                if what == "degrees":
                    for n in (0, 1):
                        dve.wait_ge(s_rec[PASSES[n][1]], 16)
                        tile_pass(n)
                    v.tensor_scalar(st2[:, :], deg["dst"][:, :], 1.0, None, ALU.add).then_inc(s_sq_in, 1)
                    inverse_root(dinv)
                elif what == "L0":
                    dve.sem_inc(s_in, 1)
                    product(0, add_bias("b_layer"))
                    dve.sem_inc(s_tab, 1)
                    attention(False, 2, 3, 1, SLOPE0, "w_a2", "w_a1", False)
                    den = acc3[:, :, D:D + 1]
                    L(v.tensor_scalar(den, den, 1e-30, None, ALU.max))
                    L(v.reciprocal(st1[:, :].unsqueeze(2), den))
                    L(v.tensor_tensor(tmp3, tmp3, nb(st1[:, :]), ALU.mult))
                    L(v.tensor_tensor(X3, X3, tmp3, ALU.add))
                    layer_norm(X3, tmp3)
                    dve.sem_inc(s_in, 1)
                elif what == "L1in":
                    product(1, add_bias("b_in"))
                elif what == "conv":
                    l = step[1]
                    dve.sem_inc(s_in, 1)
                    product(2 + l, scaled)
                    dve.sem_inc(s_tab, 1)
                    L(v.memset(acc[:, :], 0.0))
                    tile_pass(4 + l)
                    L(v.tensor_tensor(tmp3, tmp3, Y3, ALU.add))
                    L(v.tensor_tensor(tmp3, tmp3, nb(dinv[:, :]), ALU.mult))
                    L(v.tensor_tensor(tmp3, tmp3, vb(vec[f"bs{l}"][:, :]), ALU.add))
                    L(v.tensor_tensor(H3, H3, tmp3, ALU.add))
                    layer_norm(H3, tmp3, vec["gamma"][:, :], vec["beta"][:, :])
                    L(v.tensor_scalar(Hh, Hh, 0.0, None, ALU.max))
                elif what == "L1out":
                    dve.sem_inc(s_in, 1)
                    product(5, add_bias("b_out"))
                    L(v.tensor_tensor(X3, X3, Y3, ALU.add))
                    layer_norm(X3, tmp3)
                elif what == "gat":
                    l = step[1]
                    dve.sem_inc(s_in, 1)
                    product(6 + l, copied)
                    dve.sem_inc(s_tab, 1)
                    sfx = ("1", "2", "n")[l]
                    attention(True, 7 + 2 * l, 8 + 2 * l, H, SLOPE2, "as" + sfx, "ad" + sfx, True)
                elif what == "self":
                    l = step[1]
                    n_self += 1
                    dve.wait_ge(s_selfx, n_self)
                    den = acc3[:, :, D:W]
                    L(v.tensor_tensor(den, den, exs3, ALU.add))
                    L(v.tensor_scalar(den, den, GAT_EPS, None, ALU.add))
                    c = D // H
                    for h in range(H):
                        yh, ah = Y3[:, :, h * c:(h + 1) * c], acc3[:, :, h * c:(h + 1) * c]
                        L(v.tensor_tensor(yh, yh, exs3[:, :, h:h + 1].to_broadcast([P, B, c]), ALU.mult))
                        L(v.tensor_tensor(ah, ah, yh, ALU.add))
                    L(v.reciprocal(exs3, den))
                    for h in range(H):
                        ah = acc3[:, :, h * c:(h + 1) * c]
                        L(v.tensor_tensor(ah, ah, exs3[:, :, h:h + 1].to_broadcast([P, B, c]), ALU.mult))
                    L(v.tensor_tensor(H3, tmp3, vb(vec[("b1", "b2", "bn")[l]][:, :]), ALU.add))
                    if l == 2:
                        L(v.tensor_tensor(Hh, Hh, X[:, :], ALU.add))
                    L(v.tensor_scalar(Hh, Hh, 0.0, None, ALU.max))
                    if l != 1:
                        if l == 0:
                            L(v.tensor_tensor(Hh, Hh, X[:, :], ALU.add))
                        else:
                            L(v.tensor_tensor(X[:, :], Hh, X[:, :], ALU.add))
                            layer_norm(X3, tmp3)
                elif what == "gate":
                    dve.sem_inc(s_hfree, 1)
                    dve.wait_ge(s_relld, 16)
                    gr = R4[:, :, 0:D].rearrange("p q (k c) -> p q k c", k=4)
                    gwr = gw[0:EP, :].rearrange("p (c k) -> p k c", k=4)
                    for q in range(4):
                        L(v.tensor_tensor(R4t[:, q, :].rearrange("p (k c) -> p k c", k=4), gr[:, q, :, :], gwr, ALU.mult))
                    L(v.tensor_reduce(cnt[0:EP, 0:4], R4t, AX.X, ALU.add))
                    v.tensor_scalar(cnt[0:EP, 0:4], cnt[0:EP, 0:4], sc[0:EP, 2:3], None, ALU.add).then_inc(s_gz, 1)
                    dve.wait_ge(s_gs, 1)
                    L(v.tensor_scalar(cnt[0:EP, 0:4], cnt[0:EP, 0:4], 1.0, None, ALU.add))
                    L(v.reciprocal(cnt[0:EP, 0:4], cnt[0:EP, 0:4]))
                    L(v.tensor_tensor(R4[:, :, 0:D], R4[:, :, 0:D],
                                      cnt[0:EP, 0:4].unsqueeze(2).to_broadcast([EP, 4, D]), ALU.mult))
                    v.tensor_copy(R4[:, :, D:D + 1], cnt[0:EP, 0:4].unsqueeze(2)).then_inc(s_rel, 1)
                elif what == "relate":
                    v.tensor_scalar(st2[:, :], deg["src"][:, :], 1.0, None, ALU.max).then_inc(s_sq_in, 1)
                    inverse_root(dinv)
                    L(v.tensor_tensor(scaled3[:, :, 0:D], X3, nb(dinv[:, :]), ALU.mult))
                    v.tensor_copy(scaled3[:, :, D:D + 1], dinv[:, :].unsqueeze(2)).then_inc(s_tab, 1)
                    dve.wait_ge(s_tab_st, 16 * 8)
                    L(v.memset(acc[:, :], 0.0))
                    tile_pass(13)
                    dve.wait_ge(s_relst, 16)
                    v.tensor_scalar(st2[:, :], deg["dst"][:, :], 1.0, None, ALU.max).then_inc(s_sq_in, 1)
                    inverse_root(dinv)
                    L(v.tensor_tensor(H3, tmp3, nb(dinv[:, :]), ALU.mult))
                    dve.sem_inc(s_in, 1)
                    L(v.tensor_tensor(st2[:, :].unsqueeze(2), acc3[:, :, D:D + 1], dinv[:, :].unsqueeze(2), ALU.mult))
                    L(v.tensor_tensor(tmp3, vb(vec["msg_b"][:, :]), nb(st2[:, :]), ALU.mult))
                    product(9, copied)
                    L(v.tensor_tensor(H3, X3, Y3, ALU.add))
                    L(v.tensor_tensor(H3, H3, tmp3, ALU.add))
                    dve.sem_inc(s_in, 1)
                    product(10, add_bias("upd_b"))
                    for k in range(4):
                        xk = X[:, :].rearrange("p (n k) -> p n k", k=4)[:, :, k:k + 1].rearrange("p (b c) k -> p b (c k)", c=D // 4)
                        L(v.tensor_tensor(xk, xk, Y3[:, :, k * (D // 4):(k + 1) * (D // 4)], ALU.add))
                    layer_norm(X3, tmp3)
                    dve.sem_inc(s_out, 1)


PLAN = [("degrees",), ("pass", 0), ("pass", 1), ("root",),
        ("L0",), ("product", 0), ("pass", 2), ("pass", 3), ("root",),
        ("L1in",), ("product", 1),
        ("conv", 0), ("product", 2), ("pass", 4), ("root",),
        ("conv", 1), ("product", 3), ("pass", 5), ("root",),
        ("conv", 2), ("product", 4), ("pass", 6), ("root",),
        ("L1out",), ("product", 5), ("root",),
        ("gat", 0), ("product", 6), ("pass", 7), ("pass", 8), ("self", 0),
        ("gat", 1), ("product", 7), ("pass", 9), ("pass", 10), ("self", 1),
        ("gat", 2), ("product", 8), ("pass", 11), ("pass", 12), ("self", 2), ("root",),
        ("gate",), ("relate",), ("root",), ("pass", 13), ("root",), ("product", 9), ("product", 10), ("root",)]

_NAMES = ["x", "src", "dst", "edge_type_500", "L0_gnn_W_layer", "L0_gnn_b_layer", "L0_gnn_w_a1", "L0_gnn_b_a1",
          "L0_gnn_w_a2", "L0_gnn_b_a2", "L1_gnn_W_in", "L1_gnn_b_in", "L1_gnn_Ws", "L1_gnn_bs", "L1_gnn_gamma",
          "L1_gnn_beta", "L1_gnn_W_out", "L1_gnn_b_out", "L2_gnn_W1", "L2_gnn_as1", "L2_gnn_ad1", "L2_gnn_b1",
          "L2_gnn_W2", "L2_gnn_as2", "L2_gnn_ad2", "L2_gnn_b2", "L2_gnn_WN", "L2_gnn_asN", "L2_gnn_adN", "L2_gnn_bN",
          "L3_gnn_relation_emb", "L3_gnn_msg_w", "L3_gnn_msg_b", "L3_gnn_upd_w", "L3_gnn_upd_b", "L3_gnn_gate_w",
          "L3_gnn_gate_b"]


def kernel(**inputs):
    import concourse.bacc as bacc
    from concourse.bass_utils import run_bass_kernel_spmd

    nc = bacc.Bacc("TRN2", target_bir_lowering=False, num_devices=1)
    arrays, a = {}, {}
    for name in _NAMES:
        v = np.ascontiguousarray(inputs[name])
        arrays["in_" + name] = v
        a[name] = nc.dram_tensor("in_" + name, v.shape, mybir.dt.from_np(v.dtype), kind="ExternalInput").ap()
    out = nc.dram_tensor("out", (N, D), F32, kind="ExternalOutput").ap()
    row = lambda ap: ap.rearrange("a b -> (a b)")
    mats = {"w_layer": a["L0_gnn_W_layer"], "w_in": a["L1_gnn_W_in"], "ws0": a["L1_gnn_Ws"][0], "ws1": a["L1_gnn_Ws"][1],
            "ws2": a["L1_gnn_Ws"][2], "w_out": a["L1_gnn_W_out"], "w1": a["L2_gnn_W1"], "w2": a["L2_gnn_W2"],
            "wn": a["L2_gnn_WN"]}
    vecs = {"b_layer": a["L0_gnn_b_layer"], "w_a1": row(a["L0_gnn_w_a1"]), "w_a2": row(a["L0_gnn_w_a2"]),
            "b_in": a["L1_gnn_b_in"], "bs0": a["L1_gnn_bs"][0], "bs1": a["L1_gnn_bs"][1], "bs2": a["L1_gnn_bs"][2],
            "gamma": a["L1_gnn_gamma"], "beta": a["L1_gnn_beta"], "b_out": a["L1_gnn_b_out"],
            "as1": row(a["L2_gnn_as1"]), "ad1": row(a["L2_gnn_ad1"]), "b1": a["L2_gnn_b1"],
            "as2": row(a["L2_gnn_as2"]), "ad2": row(a["L2_gnn_ad2"]), "b2": a["L2_gnn_b2"],
            "asn": row(a["L2_gnn_asN"]), "adn": row(a["L2_gnn_adN"]), "bn": a["L2_gnn_bN"],
            "msg_b": row(a["L3_gnn_msg_b"]), "upd_b": row(a["L3_gnn_upd_b"])}
    gnn_program(nc, a["x"], a["src"], a["dst"], a["edge_type_500"], mats, vecs,
                [a["L0_gnn_b_a1"], a["L0_gnn_b_a2"], a["L3_gnn_gate_b"]], a["L3_gnn_relation_emb"],
                row(a["L3_gnn_gate_w"]), {"msg": a["L3_gnn_msg_w"], "upd": a["L3_gnn_upd_w"]}, out)
    r = run_bass_kernel_spmd(nc, [arrays], core_ids=[0])
    return r.results[0]["out"]
```

```python
import numpy as np
from contextlib import ExitStack

import concourse.bass as bass
from concourse import mybir

F32 = mybir.dt.float32
BF16 = mybir.dt.bfloat16
I32 = mybir.dt.int32
ALU = mybir.AluOpType
ACT = mybir.ActivationFunctionType
AX = mybir.AxisListType

P = 128
N = 3125
E = 53125
D = 256
H = 4
R = 500
B = -(-N // P)
LAST = N - (B - 1) * P
EP, EC = 125, 425
U = 8
PU = U // 2
T = -(-((E + B * (P - 1)) // P) // U) * U
PAIRS = T // 2
GROUPS = T // U
LOOP = (GROUPS - 1) // 2
PEELED = GROUPS - 2 * LOOP
USES = (GROUPS - GROUPS // 2, GROUPS // 2)
TX = T + U
W = D + H
NB = 5
DT = B // NB
SC_U = 17
SC_TURNS = EC // SC_U
STAGE_TURNS = (SC_TURNS - SC_TURNS // 2, SC_TURNS // 2)
assert SC_TURNS * SC_U == EC and SC_TURNS % 2 == 1
BANKS = {"max": 8, "plain": 8, "relate": 8, "attend": 4}
PRIME = U
BIG = 2.0 ** 100
LN_EPS = 1e-5
GAT_EPS = 1e-16
SLOPE0, SLOPE2 = 0.01, 0.2
assert EP * EC == E and DT * NB == B and T * P > E + B * (P - 1) - P and PEELED == 1

CLIFFORD = [[(0, 1), (1, 1), (2, 1), (3, -1)],
            [(1, 1), (0, 1), (3, -1), (2, 1)],
            [(2, 1), (3, 1), (0, 1), (1, -1)],
            [(3, 1), (2, 1), (1, 1), (0, 1)]]

PASSES = [("max", "src", 1, SLOPE0), ("attend", "src", 1, SLOPE0),
          ("plain", "dst", 1, 0), ("plain", "dst", 1, 0), ("plain", "dst", 1, 0),
          ("max", "dst", H, SLOPE2), ("attend", "dst", H, SLOPE2),
          ("max", "dst", H, SLOPE2), ("attend", "dst", H, SLOPE2),
          ("max", "dst", H, SLOPE2), ("attend", "dst", H, SLOPE2),
          ("relate", "dst", 1, 0)]
PRODUCTS = ["w_layer", "w_in", "ws0", "ws1", "ws2", "w_out", "w1", "w2", "wn", "msg", "upd"]
RECTIFIED = {3, 4, 5, 8}
TURNED = {"w_layer", "msg", "upd"}
VECS = ["b_layer", "w_a1", "w_a2", "b_in", "bs0", "bs1", "bs2", "gamma", "beta", "b_out",
        "as1", "ad1", "b1", "as2", "ad2", "b2", "asn", "adn", "bn", "msg_b", "upd_b"]


def before(n, *kinds):
    return sum(k in kinds for k, _, _, _ in PASSES[:n])


class Order:

    def __init__(self, eng, sem):
        self.eng, self.sem, self.n, self.i, self.per, self.k = eng, sem, 0, None, 0, 0

    def link(self, ins):
        self.mark(ins)
        self.written()

    def mark(self, ins):
        ins.then_inc(self.sem, 1)
        if self.i is None:
            self.n += 1
        else:
            self.k += 1

    def written(self, but=0):
        if self.i is None:
            self.eng.wait_ge(self.sem, self.n - but)
        else:
            self.eng.wait_ge(self.sem, self.i * self.per + (self.n + self.k - but))

    def enter(self, i, per):
        self.i, self.per, self.k = i, per, 0

    def leave(self, turns):
        assert self.k == self.per, (self.k, self.per)
        self.n += turns * self.per
        self.i = None


def gnn_program(nc, x, src, dst, etype, mats, vecs, scalars, relation, gate_w, clif_w, out):
    ctx = ExitStack()
    with ctx:
        def sb(name, shape, dt=F32):
            return ctx.enter_context(nc.sbuf_tensor(name, shape, dt))

        def sem(name):
            return ctx.enter_context(nc.semaphore(name))

        table = nc.dram_tensor("node_table", (B * P, D), F32).ap()
        table3 = nc.dram_tensor("node_table_scaled", (B * P, D + 1), F32).ap()
        score_table = nc.dram_tensor("score_table", (B * P, H), F32).ap()
        rel_table = nc.dram_tensor("relation_table", (R, D + 1), F32).ap()
        records = {o: nc.dram_tensor(f"records_{o}", (P * T, 4), I32).ap() for o in ("src", "dst")}

        X = sb("X", [P, B * D])
        HY = sb("HY", [P, 2 * B * D])
        Hh = HY[:, 0:B * D]
        Y = HY[:, B * D:2 * B * D]
        acc = sb("acc", [P, B * W])
        acc3 = acc[:, :].rearrange("p (b w) -> p b w", w=W)
        tmp3 = acc3[:, :, 0:D]
        rec = {o: sb(f"rec_{o}", [P, TX * 4], I32) for o in ("src", "dst")}
        block_of = {o: sb(f"block_of_{o}", [P, T + U], I32) for o in ("src", "dst")}
        ES = sb("ES", [P, TX * H])
        G = sb("G", [P, 2 * U, D + 1])
        M = Hh[:, 0:2 * U * W].rearrange("p (u w) -> p u w", w=W)
        OHA = sb("OHA", [P, 3 * U * P])
        OH = OHA[:, 0:2 * U * P].rearrange("p (u n) -> p u n", n=P)
        OHB = OHA[:, 2 * U * P:].bitcast(BF16)
        OHC = OHB[:, 0:U * P].rearrange("p (u n) -> p u n", n=P)
        OHT = OHB[:, U * P:2 * U * P].rearrange("p (u n) -> p u n", n=P)
        NE = OH[:, :, :].rearrange("p u n -> p (u n)").bitcast(BF16)[:, 0:2 * U * P].rearrange("p (u n) -> p u n", n=P)
        XS = [OHA[:, g * NB * D:(g + 1) * NB * D] for g in range(2)]
        XT = [G[:, :, :].rearrange("p u d -> p (u d)")[:, g * NB * D:(g + 1) * NB * D] for g in range(2)]
        wbuf = sb("wbuf", [P, 2, 2, D])
        wraw = sb("wraw", [P, 2, D])
        vec = {n: sb(f"v_{n}", [P, D]) for n in VECS}
        sc = sb("scal", [P, 3])
        ESN = sb("ESN", [P, B * H])
        EDM = sb("EDM", [P, B * 2 * H])
        MX = sb("MX", [P, B * H])
        ident_b = sb("ident_b", [P, P], BF16)
        EDB = sb("EDB", [P, B * 3 * 2 * H], BF16)
        target = sb("target", [P, U, 3 * 2 * H], BF16)
        left = sb("left", [P, B * 2 * H])
        edge_max = sb("edge_max", [P, U, H])
        SC = sb("SC", [P, U * H])
        EX = sb("EX", [P, 2, U * H])
        exs = sb("exs", [P, B * H])
        st1 = sb("st1", [P, B])
        st2 = sb("st2", [P, B])
        deg = {o: sb(f"deg_{o}", [P, B]) for o in ("src", "dst")}
        dinv = sb("dinv", [P, B])
        ident = sb("ident", [P, P])
        zero = sb("zero", [P, 1])
        ones = sb("ones", [P, P])
        before_me = sb("before_me", [P, P])
        iota_n = sb("iota_n", [P, P])
        neg_ident = sb("neg_ident", [P, H, P], BF16)
        iota_i = sb("iota_i", [P, T], I32)
        gw = sb("gw", [P, D])
        cnt = sb("cnt", [P, B])
        cnt2 = sb("cnt2", [P, B])
        cnt_i = sb("cnt_i", [P, B], I32)
        base = sb("base", [P, B])
        stage = sb("stage", [P, 2, SC_U * 4], I32)
        idx = sb("idx", [P, 2 * SC_U], I32)
        rows = sb("rows", [P, 2 * U, 2], I32)

        A = acc[:, :]
        S_scan = HY[0:EP, 0:B * EC]
        S_src, S_dst, S_typ, S_i = (A[0:EP, n * EC:(n + 1) * EC].bitcast(I32) for n in range(4))
        S_q, S_f, S_pos, S_zero = (A[0:EP, (4 + n) * EC:(5 + n) * EC] for n in range(4))
        S_recf = {"src": HY[0:EP, B * EC:(B + 4) * EC], "dst": A[0:EP, 8 * EC:12 * EC]}
        S_rec = {o: ap.bitcast(I32) for o, ap in S_recf.items()}
        S_adr = {"src": HY[0:EP, (B + 4) * EC:(B + 5) * EC].bitcast(I32), "dst": A[0:EP, 12 * EC:13 * EC].bitcast(I32)}
        assert 13 * EC <= B * W and (B + 5) * EC <= 2 * B * D
        HOT = G[0:EP, :, :].rearrange("p u d -> p (u d)").bitcast(BF16)

        def hot_low(g):
            return HOT[:, g * SC_U * P:(g + 1) * SC_U * P].rearrange("p (c n) -> p c n", n=P)

        def hot_block(g):
            at = (2 * P + g * B) * SC_U
            return HOT[:, at:at + SC_U * B].rearrange("p (c n) -> p c n", n=B)

        assert 2 * (P + B) * SC_U <= 2 * 2 * U * (D + 1)
        fill = G[:, :, :].rearrange("p u d -> p (u d)")[:, 0:T * 4]
        assert T * 4 <= 2 * U * (D + 1) and 2 * T <= U * P
        iota_t = OHA[:, 2 * U * P:2 * U * P + T]
        bt_f = OHA[:, 2 * U * P + T:2 * U * P + 2 * T]

        ps = ctx.enter_context(nc.psum_tensor("ps", [P, 8, 512], F32))
        psf = ps[:, :, :].rearrange("p b n -> p (b n)")
        T_ps = psf[:, 4 * 512:5 * 512].bitcast(BF16)
        EDM_ps = ps[:, 6, 0:U * 2 * H]
        XT_ps = psf[:, 0:NB * D]
        Y_ps = psf[:, 3 * 512:3 * 512 + NB * D]

        s_load, s_const, s_order, s_gorder = sem("loaded"), sem("constants"), sem("dve_order"), sem("pool_order")
        s_cnt, s_offs, s_fill, s_filled, s_adr = (sem(n) for n in (
            "counts_ready", "offsets_ready", "fill_ready", "filled", "addresses_ready"))
        s_in, s_xs, s_xt_ps, s_xt, s_y_ps, s_y = (sem(n) for n in (
            "product_input", "xs_ready", "xt_in_psum", "xt_ready", "y_in_psum", "y_ready"))
        s_wraw, s_wT_ps, s_wT, s_kneg, s_kraw = (sem(n) for n in (
            "raw_weight_loaded", "weight_turned", "weight_ready", "clifford_signed", "clifford_loaded"))
        s_w = [sem(f"weight_loaded{k}") for k in range(2)]
        s_sorted = [sem(f"sorted{k}") for k in range(2)]
        s_rec = {o: sem(f"records_loaded_{o}") for o in ("src", "dst")}
        s_hot, s_hist, s_seed, s_acc, s_target, s_loadx = (sem(n) for n in (
            "degree_rows_ready", "degrees_counted", "sums_seeded", "sums_free", "targets_staged", "nodes_loaded"))
        s_ohc = sem("bf16_rows_ready")
        s_rows = sem("gather_rows_ready")
        s_centred, s_squared = sem("blocks_centred"), sem("blocks_squared")
        s_den = sem("denominator_weights_ready")
        s_idx = sem("indices_ready")
        s_sq_in, s_sq = sem("root_input"), sem("root_ready")
        s_hfree, s_relld = sem("h_free"), sem("relation_loaded")
        landed = [sem(f"landed{q}") for q in range(U)]
        rel_landed = [sem(f"rel_landed{q}") for q in range(U)]
        s_oh, s_ps, s_psfree, s_msg = (sem(n) for n in (
            "onehot_ready", "sum_in_psum", "psum_free", "message_ready"))
        s_T, s_OHT, s_edm, s_sc, s_ex = (sem(n) for n in (
            "turned_in_psum", "turned_ready", "target_scores_ready", "scores_ready", "exp_ready"))
        s_tab_sc, s_tab, s_stab_st, s_tab_st = (sem(n) for n in (
            "score_table_ready", "table_ready", "score_table_stored", "table_stored"))
        s_self, s_selfx, s_rel, s_relst, s_gz, s_gs, s_out, s_fin = (sem(n) for n in (
            "self_scores_ready", "self_exp_ready", "relation_rows_ready", "relation_stored",
            "gate_sum_ready", "gate_ready", "output_ready", "stored"))

        tab_view = table.rearrange("(b p) d -> p b d", p=P)
        tab3_view = table3.rearrange("(b p) d -> p b d", p=P)
        stab_view = score_table.rearrange("(b p) d -> p b d", p=P)
        Y3 = Y.rearrange("p (b d) -> p b d", d=D)
        H3 = Hh.rearrange("p (b d) -> p b d", d=D)
        X3 = X[:, :].rearrange("p (b d) -> p b d", d=D)
        scaled3 = acc[:, 0:B * (D + 1)].rearrange("p (b d) -> p b d", d=D + 1)
        R4 = Hh[0:EP, 0:4 * (D + 1)].rearrange("p (q d) -> p q d", d=D + 1)
        R4t = Y[0:EP, 0:4 * D].rearrange("p (q d) -> p q d", d=D)

        def load_blocks(eng, o, at, count):
            _, regs = nc.values_load_multi_w_load_instructions(
                block_of[o][0:1, bass.ds(at, count)], engines=(eng.engine,), min_val=0, max_val=B - 1,
                skip_runtime_bounds_check_because="a block number counts at most B - 1 comparisons")
            return regs

        RAW_LOADS = 2 + len(VECS) + 3 + 1
        block = ctx.enter_context(nc.Block())

        @block.sync
        def _(sp):
            def load_weight(j):
                name = PRODUCTS[j]
                if j >= 2:
                    sp.wait_ge(s_y_ps, 1 + DT * (j - 1))
                if name in ("msg", "upd"):
                    sp.wait_ge(s_wT_ps, 1 if name == "msg" else 2)
                    for i in range(4):
                        for jj, (w, _) in enumerate(CLIFFORD[i]):
                            sp.dma_start(wraw[64 * (i % 2):64 * (i % 2) + 64, i // 2, 64 * jj:64 * jj + 64],
                                         clif_w[name][w, :, :]).then_inc(s_kraw, 16)
                elif name in TURNED:
                    sp.dma_start(wraw[:, :, :], mats[name].rearrange("(k p) n -> p k n", p=P)).then_inc(s_wraw, 16)
                else:
                    sp.dma_start(wbuf[:, j % 2, :, :], mats[name].rearrange("(k p) n -> p k n", p=P)).then_inc(s_w[j % 2], 16)

            sp.dma_start(S_src, src.rearrange("(p c) -> p c", c=EC)).then_inc(s_load, 16)
            sp.dma_start(S_dst, dst.rearrange("(p c) -> p c", c=EC)).then_inc(s_load, 16)
            sp.dma_start(S_typ, etype.rearrange("(p c) -> p c", c=EC)).then_inc(s_load, 16)
            sp.wait_ge(s_fill, 1)
            for o in ("src", "dst"):
                sp.dma_start(records[o].rearrange("(p t) f -> p (t f)", p=P), fill.bitcast(I32)).then_inc(s_filled, 16)
            sp.wait_ge(s_const, 1)
            sp.dma_start(X3[:, 0:B - 1, :], x[0:(B - 1) * P, :].rearrange("(b p) d -> p b d", p=P)).then_inc(s_loadx, 16)
            sp.dma_start(X3[0:LAST, B - 1, :], x[(B - 1) * P:N, :]).then_inc(s_loadx, 16)
            for n in VECS:
                sp.dma_start(vec[n][:, :], vecs[n].partition_broadcast(P)).then_inc(s_loadx, 16)
            for n in range(3):
                sp.dma_start(sc[:, n:n + 1], scalars[n].partition_broadcast(P)).then_inc(s_loadx, 16)
            sp.dma_start(gw[:, :], gate_w.partition_broadcast(P)).then_inc(s_loadx, 16)
            load_weight(0)
            load_weight(1)
            for n, o in enumerate(("src", "dst")):
                for s_, turns in zip(s_sorted, STAGE_TURNS):
                    sp.wait_ge(s_, 16 * SC_U * turns * (n + 1))
                sp.dma_start(rec[o][:, 0:T * 4], records[o].rearrange("(p t) f -> p (t f)", p=P)).then_inc(s_rec[o], 16)

            def store_tables(stage):
                sp.wait_ge(s_tab_sc, stage)
                sp.dma_start(stab_view, ESN[:, :].rearrange("p (b h) -> p b h", h=H)).then_inc(s_stab_st, 16)

            score_stage = 0
            for n in range(7):
                j = (0, 2, 3, 4, 6, 7, 8)[n]
                if n == 0 or n >= 4:
                    score_stage += 1
                    store_tables(score_stage)
                sp.wait_ge(s_tab, n + 1)
                sp.dma_start(tab_view, Y3).then_inc(s_tab_st, 16)
                for jj in {0: (2,), 1: (3,), 2: (4,), 3: (5, 6), 4: (7,), 5: (8,), 6: (9,)}[n]:
                    load_weight(jj)
            sp.wait_ge(s_hfree, 1)
            sp.dma_start(R4[:, :, 0:D], relation.rearrange("(q p) d -> p q d", p=EP)).then_inc(s_relld, 16)
            sp.wait_ge(s_rel, 1)
            sp.dma_start(rel_table.rearrange("(q p) d -> p q d", p=EP), R4).then_inc(s_relst, 16)
            sp.wait_ge(s_tab, 8)
            sp.dma_start(tab3_view, scaled3).then_inc(s_tab_st, 16)
            load_weight(10)
            sp.wait_ge(s_out, 1)
            sp.dma_start(out[0:(B - 1) * P, :].rearrange("(b p) d -> p b d", p=P), X3[:, 0:B - 1, :]).then_inc(s_fin, 16)
            sp.dma_start(out[(B - 1) * P:N, :], X3[0:LAST, B - 1, :]).then_inc(s_fin, 16)
            sp.wait_ge(s_fin, 32)

        @block.gpsimd
        def _(pool):
            order = Order(pool, s_gorder)
            pool.memset(X3[:, B - 1, :], 0.0).then_inc(s_const, 1)
            order.link(pool.memset(ident[:, :], 0.0))
            order.link(pool.affine_select(out=ident[:, :], in_=ident[:, :], compare_op=ALU.not_equal, fill=1.0,
                                          base=0, pattern=[[-1, P]], channel_multiplier=1))
            order.link(pool.memset(ones[:, :], 1.0))
            order.link(pool.affine_select(out=before_me[:, :], in_=ones[:, :], compare_op=ALU.is_gt, fill=0.0,
                                          base=0, pattern=[[1, P]], channel_multiplier=-1))
            pool.iota(iota_i[:, :], pattern=[[1, T]], base=0, channel_multiplier=0).then_inc(s_const, 1)

            pool.wait_ge(s_filled, 32)
            for n, o in enumerate(("src", "dst")):
                pool.wait_ge(s_adr, n + 1)

                def turn(t, st, past):
                    served = STAGE_TURNS[st] * n + past
                    if not (isinstance(served, int) and served == 0):
                        pool.wait_ge(s_sorted[st], served * (16 * SC_U))
                    pool.tensor_copy(idx[0:EP, st * SC_U:(st + 1) * SC_U], S_adr[o][:, bass.ds(t * SC_U, SC_U)]).then_inc(s_idx, 1)
                    pool.tensor_copy(stage[0:EP, st, :], S_rec[o][:, bass.ds(t * (SC_U * 4), SC_U * 4)]).then_inc(s_idx, 1)
                    pool.wait_ge(s_idx, t * 2 + (2 * n * SC_TURNS + 2))
                    pool.nop(nofuse=True)
                    for k in range(SC_U):
                        pool.indirect_dma_start(
                            out=records[o][:, :],
                            out_offset=bass.IndirectOffsetOnAxis(ap=idx[0:EP, st * SC_U + k:st * SC_U + k + 1], axis=0),
                            in_=stage[0:EP, st, 4 * k:4 * k + 4], in_offset=None).then_inc(s_sorted[st], 16)

                turn(0, 0, 0)
                turn(1, 1, 0)
                turn(2, 0, 1)
                with pool.Fori(0, (SC_TURNS - 3) // 2) as i:
                    turn(i * 2 + 3, 1, i + 1)
                    turn(i * 2 + 4, 0, i + 2)

            def gather(n, dest, tab, col, sems, use):

                def group(i, g):
                    pool.wait_ge(s_rows, i * 2 + (use * (GROUPS + 1) + g + 1))
                    pool.nop(nofuse=True)
                    for k in range(g * U, (g + 1) * U):
                        for d_, t_, c_, s_ in zip(dest, tab, col, sems):
                            pool.indirect_dma_start(
                                out=d_(k), out_offset=None, in_=t_,
                                in_offset=bass.IndirectOffsetOnAxis(
                                    ap=rows[:, k, c_:c_ + 1], axis=0)).then_inc(s_[k // 2], 16)

                with pool.Fori(0, LOOP) as i:
                    group(i, 0)
                    group(i, 1)
                group(LOOP, 0)

            for o in ("src", "dst"):
                pool.wait_ge(s_rec[o], 16)
            tables = scores = 0
            for n, (kind, o, heads, _) in enumerate(PASSES):
                use = before(n, "max", "attend", "plain", "relate")
                if kind == "max":
                    scores += 1
                    pool.wait_ge(s_stab_st, 16 * scores)
                    gather(n, [lambda k: G[:, k, 0:H]], [score_table[:, :]], [0], [landed], use)
                elif kind in ("attend", "plain"):
                    tables += 1
                    pool.wait_ge(s_tab_st, 16 * tables)
                    gather(n, [lambda k: G[:, k, 0:D]], [table[:, :]], [0], [landed], use)
                elif kind == "relate":
                    pool.wait_ge(s_tab_st, 16 * (tables + 1))
                    pool.wait_ge(s_relst, 16)
                    gather(n, [lambda k: G[:, k, :], lambda k: M[:, k, 0:D + 1]], [table3[:, :], rel_table[:, :]],
                           [0, 1], [landed, rel_landed], use)

        @block.tensor
        def _(pe):
            def offsets(n):
                pe.wait_ge(s_const, 2)
                pe.wait_ge(s_cnt, n + 1)
                nc.tensor.matmul(ps[0:EP, 0, 0:B], before_me[0:EP, 0:EP], cnt[0:EP, :], start=True, stop=True)
                nc.tensor.matmul(ps[:, 1, 0:B], ones[0:EP, :], cnt[0:EP, :], start=True, stop=True).then_inc(s_offs, 1)

            turned = [0]

            def turn_weight(j):
                name = PRODUCTS[j]
                if name not in TURNED:
                    return
                if name == "w_layer":
                    pe.wait_ge(s_wraw, 16)
                else:
                    pe.wait_ge(s_kneg, turned[0])
                for k in range(2):
                    for m in range(2):
                        last = nc.tensor.transpose(ps[:, 6 + k, m * P:(m + 1) * P], wraw[:, m, k * P:(k + 1) * P], ident[:, :])
                last.then_inc(s_wT_ps, 1)
                turned[0] += 1

            loaded = [0, 0]

            def product(j):
                turn_weight(j)
                if PRODUCTS[j] in TURNED:
                    pe.wait_ge(s_wT, turned[0])
                else:
                    loaded[j % 2] += 1
                    pe.wait_ge(s_w[j % 2], 16 * loaded[j % 2])

                def turn_input(t, g):
                    pe.wait_ge(s_xs, t + (DT * j + 1))
                    pe.wait_ge(s_xt, t + DT * j)
                    for q in range(2 * NB):
                        last = nc.tensor.transpose(XT_ps[:, q * P:(q + 1) * P], XS[g][:, q * P:(q + 1) * P], ident[:, :])
                    last.then_inc(s_xt_ps, 1)

                def multiply(t, g):
                    pe.wait_ge(s_xt, t + (DT * j + 1))
                    pe.wait_ge(s_y, t + (1 + DT * j))
                    for q in range(NB):
                        for k in range(2):
                            last = nc.tensor.matmul(Y_ps[:, q * D:(q + 1) * D], XT[g][:, (2 * q + k) * P:(2 * q + k + 1) * P],
                                                    wbuf[:, j % 2, k, :], start=(k == 0), stop=(k == 1))
                    last.then_inc(s_y_ps, 1)

                turn_input(0, 0)
                with pe.Fori(0, DT // 2) as i:
                    turn_input(i * 2 + 1, 1)
                    multiply(i * 2, 0)
                    turn_input(i * 2 + 2, 0)
                    multiply(i * 2 + 1, 1)
                multiply(DT - 1, 0)

            def tile_pass(n):
                kind, o, heads, _ = PASSES[n]
                use = before(n, "max", "attend", "plain", "relate")
                att, msg = before(n, "attend"), before(n, "attend", "relate")

                def turn_rows(i, ahead, g):
                    pe.wait_ge(s_ohc, i * 2 + (att * (GROUPS + 1) + ahead + 1))
                    if ahead:
                        pe.wait_ge(s_OHT, i * 2 + (att * (GROUPS + 1) + ahead))
                    for k in range(U):
                        last = nc.tensor.transpose(T_ps[:, k * P:(k + 1) * P], OHC[:, k, :], ident_b[:, :])
                    last.then_inc(s_T, 1)

                def target_scores(i, ahead):
                    pe.wait_ge(s_OHT, i * 2 + (att * (GROUPS + 1) + ahead + 1))
                    pe.wait_ge(s_target, i * 2 + (att * (GROUPS + 1) + ahead + 1))
                    if ahead:
                        pe.wait_ge(s_sc, i * 2 + (att * (GROUPS + 1) + ahead))
                    for k in range(U):
                        for part in range(3):
                            last = nc.tensor.matmul(EDM_ps[:, k * 2 * H:(k + 1) * 2 * H], OHT[:, k, :],
                                                    target[:, k, part * 2 * H:(part + 1) * 2 * H],
                                                    start=(part == 0), stop=(part == 2))
                    last.then_inc(s_edm, 1)

                def sums(i, g, tiles):
                    for k in tiles:
                        pe.wait_ge(s_psfree, i * (2 * U) + (PRIME - BANKS[kind] + n * T + g * U + k + 1))
                        bank, s = k % BANKS[kind], g * U + k
                        if kind in ("max", "plain"):
                            if k % 2 == 0:
                                pe.wait_ge(landed[s // 2], i * 32 + 32 * (use * USES[g] + 1))
                        elif k % 2 == 0:
                            pe.wait_ge(s_msg, i * (2 * PU) + (msg * PAIRS + g * PU + k // 2 + 1))
                        if kind == "max":
                            nc.tensor.matmul(ps[:, bank, 0:heads * P], NE[:, s, :],
                                             neg_ident[:, 0:heads, :], start=True, stop=False)
                            for h in range(heads):
                                last = nc.tensor.matmul(ps[:, bank, h * P:(h + 1) * P], G[:, s, h:h + 1].to_broadcast([P, P]),
                                                        ident[:, :], start=False, stop=(h == heads - 1))
                        elif kind == "plain":
                            last = nc.tensor.matmul(ps[:, bank, 0:D], OH[:, s, :], G[:, s, 0:D], start=True, stop=True)
                        else:
                            w = W if heads == H else D + 1
                            last = nc.tensor.matmul(ps[:, bank, 0:w], OH[:, s, :], M[:, s, 0:w], start=True, stop=True)
                        last.then_inc(s_ps, 1)

                def group(i, g):
                    if kind != "attend":
                        pe.wait_ge(s_oh, i * 2 + (n * (GROUPS + 1) + g + 1))
                        sums(i, g, range(U))
                    else:
                        pe.wait_ge(s_den, i * 2 + (att * (GROUPS + 1) + g + 1))
                        sums(i, g, range(4))
                        turn_rows(i, g + 1, 1 - g)
                        sums(i, g, range(4, U - 2))
                        target_scores(i, g + 1)
                        sums(i, g, range(U - 2, U))

                if kind == "attend":
                    turn_rows(0, 0, 0)
                    target_scores(0, 0)
                with pe.Fori(0, LOOP) as i:
                    group(i, 0)
                    group(i, 1)
                group(LOOP, 0)

            def histogram(n):
                def turn(t, g, first=False, last=False):
                    pe.wait_ge(s_hot, t + (n * SC_TURNS + 1))
                    for k in range(SC_U):
                        ins = nc.tensor.matmul(ps[:, 5, 0:B], hot_low(g)[:, k, :], hot_block(g)[:, k, :],
                                               start=first and k == 0, stop=last and k == SC_U - 1)
                    ins.then_inc(s_hist, 1)

                turn(0, 0, first=True)
                with pe.Fori(0, SC_TURNS // 2 - 1) as i:
                    turn(i * 2 + 1, 1)
                    turn(i * 2 + 2, 0)
                turn(SC_TURNS - 2, 1)
                turn(SC_TURNS - 1, 0, last=True)

            for n in range(2):
                offsets(n)
                histogram(n)
            for step in PLAN:
                product(step[1]) if step[0] == "product" else tile_pass(step[1]) if step[0] == "pass" else None

        @block.scalar
        def _(act):
            turned = [0]

            def product(j):
                name = PRODUCTS[j]
                if name in TURNED:
                    if name != "w_layer":
                        act.wait_ge(s_kraw, 16 * 16 * turned[0])
                        negs = [(i, jj) for i in range(4) for jj in range(4) if CLIFFORD[i][jj][1] < 0]
                        for i, jj in negs:
                            w = wraw[64 * (i % 2):64 * (i % 2) + 64, i // 2, 64 * jj:64 * jj + 64]
                            last = nc.scalar.mul(w, w, -1.0)
                        last.then_inc(s_kneg, 1)
                    turned[0] += 1
                    act.wait_ge(s_wT_ps, turned[0])
                    nc.scalar.copy(wbuf[:, j % 2, :, :], ps[:, 6:8, 0:D]).then_inc(s_wT, 1)
                source = X if name in ("w_layer", "w_in", "w1") else HY
                rectify = j in RECTIFIED

                def take(t):
                    act.wait_ge(s_in, DT * j + t + 1)
                    act.wait_ge(s_xt_ps, 1 + DT * j + max(t - 1, 0))
                    nc.scalar.activation(XS[t % 2], source[:, t * NB * D:(t + 1) * NB * D],
                                         ACT.Relu if rectify else ACT.Copy).then_inc(s_xs, 1)

                take(0)
                for t in range(DT):
                    if t + 1 < DT:
                        take(t + 1)
                    act.wait_ge(s_xt_ps, 1 + DT * j + t + 1)
                    act.wait_ge(s_y_ps, 1 + DT * j + max(t - 1, 0))
                    nc.scalar.copy(XT[t % 2], XT_ps).then_inc(s_xt, 1)
                    if name[:2] == "ws" and t:
                        seed(j, t - 1)
                if name[:2] == "ws":
                    seed(j, DT - 1)

            def seed(j, t):
                act.wait_ge(s_y, 1 + DT * j + t + 1)
                ins = nc.scalar.copy(acc3[:, t * NB:(t + 1) * NB, 0:D], Y3[:, t * NB:(t + 1) * NB, :])
                if t == DT - 1:
                    ins.then_inc(s_seed, 1)

            def tile_pass(n):
                kind, o, _, _ = PASSES[n]
                att = before(n, "attend")
                recs = rec[o][:, :].rearrange("p (t f) -> p t f", f=4)

                def gather_rows(i, ahead, g):
                    act.wait_ge(s_psfree, i * (2 * U) + (PRIME + n * T + max(ahead - 1, 0) * U))
                    for c in range(2 if kind == "relate" else 1):
                        ins = nc.scalar.copy(rows[:, g * U:(g + 1) * U, c:c + 1],
                                             recs[:, bass.ds((i * 2 + ahead) * U, U), 2 * c:2 * c + 1])
                    ins.then_inc(s_rows, 1)

                def look_ahead(i, ahead, g):
                    act.wait_ge(s_oh, i * 2 + (n * (GROUPS + 1) + ahead + 1))
                    nc.scalar.copy(OHC, OH[:, g * U:(g + 1) * U, :]).then_inc(s_ohc, 1)
                    act.wait_ge(s_T, i * 2 + (att * (GROUPS + 1) + ahead + 1))
                    if ahead:
                        act.wait_ge(s_edm, i * 2 + (att * (GROUPS + 1) + ahead))
                    nc.scalar.copy(OHT[:, :, :].rearrange("p u n -> p (u n)"), T_ps).then_inc(s_OHT, 1)
                    act.wait_ge(s_sc, i * 2 + (att * (GROUPS + 1) + ahead + 1))
                    if ahead:
                        act.wait_ge(s_msg, i * (2 * PU) + (att * PAIRS + (ahead - 1) * PU))
                    nc.scalar.activation(EX[:, g, :], SC[:, :], ACT.Exp).then_inc(s_ex, 1)
                    nc.scalar.activation(M[:, g * U:(g + 1) * U, D:D + H], SC[:, :].rearrange("p (u h) -> p u h", h=H),
                                         ACT.Exp).then_inc(s_den, 1)

                act.wait_ge(s_rec[o], 16)
                if n:
                    act.wait_ge(s_rows, n * (GROUPS + 1))
                gather_rows(0, 0, 0)
                if kind == "attend":
                    look_ahead(0, 0, 0)

                def group(i, g):
                    gather_rows(i, g + 1, 1 - g)
                    if kind == "attend":
                        look_ahead(i, g + 1, 1 - g)

                with act.Fori(0, LOOP) as i:
                    group(i, 0)
                    group(i, 1)
                group(LOOP, 0)

            n_self = roots = n_zero = n_square = 0
            for step in PLAN:
                if step[0] == "product":
                    product(step[1])
                elif step[0] == "pass":
                    tile_pass(step[1])
                elif step[0] == "zero":
                    n_zero += 1
                    act.wait_ge(s_acc, n_zero)
                    nc.scalar.copy(acc[:, :], zero[:, 0:1].to_broadcast([P, B * W])).then_inc(s_seed, 1)
                elif step[0] == "self":
                    n_self += 1
                    act.wait_ge(s_self, n_self)
                    nc.scalar.activation(exs[:, :], exs[:, :], ACT.Exp).then_inc(s_selfx, 1)
                elif step[0] == "square":
                    for t in range(DT):
                        n_square += 1
                        act.wait_ge(s_centred, n_square)
                        nc.scalar.activation(tmp3[:, t * NB:(t + 1) * NB, :], (X3 if step[1] == "X" else H3)[:, t * NB:(t + 1) * NB, :],
                                             ACT.Square).then_inc(s_squared, 1)
                elif step[0] == "root":
                    roots += 1
                    act.wait_ge(s_sq_in, roots)
                    nc.scalar.activation(st2[:, :], st2[:, :], ACT.Sqrt).then_inc(s_sq, 1)
                elif step[0] == "gate":
                    act.wait_ge(s_gz, 1)
                    nc.scalar.activation(cnt[0:EP, 0:4], cnt[0:EP, 0:4], ACT.Exp, scale=-1.0).then_inc(s_gs, 1)

        @block.vector
        def _(dve):
            order = Order(dve, s_order)
            L = order.link
            v = nc.vector
            nb = lambda ap, w=D: ap.unsqueeze(2).to_broadcast([P, B, w])
            vb = lambda ap: ap.unsqueeze(1).to_broadcast([P, B, D])

            def sort(n, o):
                key, other = (S_src, S_dst) if o == "src" else (S_dst, S_src)
                adr, recf = S_adr[o], S_recf[o].rearrange("p (c f) -> p c f", f=4)
                L(v.tensor_scalar(S_i, key, 7, None, ALU.logical_shift_right))
                L(v.tensor_copy(S_q, S_i))
                L(v.tensor_scalar(S_i, key, P - 1, None, ALU.bitwise_and))
                r = S_rec[o].rearrange("p (c f) -> p c f", f=4)
                v.tensor_copy(recf[:, :, 1:2], S_i.unsqueeze(2))
                v.tensor_copy(r[:, :, 0:1], other.unsqueeze(2))
                v.tensor_copy(r[:, :, 2:3], S_typ.unsqueeze(2))
                v.memset(r[:, :, 3:4], 0)
                L(v.memset(S_zero, 0.0))
                with dve.Fori(0, B) as b:
                    order.enter(b, 2)
                    L(v.tensor_scalar(S_f, S_q, iota_n[0:EP, bass.ds(b, 1)], None, ALU.is_equal))
                    L(v.tensor_tensor_scan(S_scan[:, bass.ds(b * EC, EC)], S_f, S_zero, 0.0, ALU.add, ALU.add))
                    order.leave(B)
                scan3 = S_scan.rearrange("p (b c) -> p b c", c=EC)
                v.tensor_copy(cnt[0:EP, :].unsqueeze(2), scan3[:, :, EC - 1:EC]).then_inc(s_cnt, 1)
                dve.wait_ge(s_offs, n + 1)
                L(v.tensor_scalar(cnt_i[:, :], ps[:, 1, 0:B], float(P - 1), None, ALU.add))
                L(v.tensor_scalar(cnt_i[:, :], cnt_i[:, :], 7, None, ALU.logical_shift_right))
                L(v.tensor_copy(cnt2[:, :], cnt_i[:, :]))
                L(v.tensor_tensor_scan(base[:, :], cnt2[:, :], nul_b, 0.0, ALU.add, ALU.add))
                L(v.tensor_tensor(cnt2[:, :], base[:, :], cnt2[:, :], ALU.subtract))
                L(v.scalar_tensor_tensor(base[0:EP, :], cnt2[0:EP, :], float(P), ps[0:EP, 0, 0:B], ALU.mult, ALU.add))
                L(v.tensor_scalar(base[0:EP, :], base[0:EP, :], -1.0, None, ALU.add))
                L(v.tensor_tensor(scan3, scan3, base[0:EP, :].unsqueeze(2).to_broadcast([EP, B, EC]), ALU.add))
                L(v.memset(S_pos, 0.0))
                with dve.Fori(0, B) as b:
                    order.enter(b, 2)
                    L(v.scalar_tensor_tensor(S_f, S_q, iota_n[0:EP, bass.ds(b, 1)], S_scan[:, bass.ds(b * EC, EC)],
                                             ALU.is_equal, ALU.mult))
                    L(v.tensor_tensor(S_pos, S_pos, S_f, ALU.add))
                    order.leave(B)
                L(v.tensor_copy(adr, S_pos))
                L(v.tensor_scalar(S_i, adr, P - 1, None, ALU.bitwise_and))
                L(v.tensor_scalar(adr, adr, 7, None, ALU.logical_shift_right))
                L(v.tensor_copy(S_f, S_i))
                L(v.tensor_copy(S_pos, adr))
                L(v.scalar_tensor_tensor(S_f, S_f, float(T), S_pos, ALU.mult, ALU.add))
                v.tensor_copy(adr, S_f).then_inc(s_adr, 1)
                v.tensor_copy(iota_t, iota_i[:, 0:T])
                L(v.memset(bt_f, 0.0))
                with dve.Fori(0, B - 1) as b:
                    order.enter(b, 1)
                    L(v.scalar_tensor_tensor(bt_f, iota_t, cnt2[:, bass.ds(b + 1, 1)], bt_f, ALU.is_ge, ALU.add))
                    order.leave(B - 1)
                L(v.tensor_copy(block_of[o][:, 0:T], bt_f))

            def degrees(n, o):
                local = S_recf[o].rearrange("p (c f) -> p c f", f=4)

                def turn(t, g):
                    if not (isinstance(t, int) and t == 0):
                        dve.wait_ge(s_hist, t + n * SC_TURNS)
                    v.tensor_tensor(hot_low(g), iota_n[0:EP, :].unsqueeze(1).to_broadcast([EP, SC_U, P]),
                                    local[:, bass.ds(t * SC_U, SC_U), 1:2].to_broadcast([EP, SC_U, P]), ALU.is_equal)
                    v.tensor_tensor(hot_block(g), iota_n[0:EP, 0:B].unsqueeze(1).to_broadcast([EP, SC_U, B]),
                                    S_q[:, bass.ds(t * SC_U, SC_U)].unsqueeze(2).to_broadcast([EP, SC_U, B]),
                                    ALU.is_equal).then_inc(s_hot, 1)

                turn(0, 0)
                with dve.Fori(0, SC_TURNS // 2) as i:
                    turn(i * 2 + 1, 1)
                    turn(i * 2 + 2, 0)
                dve.wait_ge(s_hist, 1 + (n + 1) * SC_TURNS)
                L(v.tensor_copy(deg[o][:, :], ps[:, 5, 0:B]))

            def product(j, finish, feed=None, after=None):
                def take_out(t):
                    dve.wait_ge(s_y_ps, t + (1 + DT * j + 1))
                    finish({1: Hh, 5: X}.get(j, Y), t).then_inc(s_y, 1)

                if feed is None and after is None:
                    with dve.Fori(0, DT) as i:
                        take_out(i)
                else:
                    for t in range(DT + 2):
                        if feed is not None and t < DT:
                            feed(t)
                        if t >= 2:
                            take_out(t - 2)
                            if after is not None:
                                dve.wait_ge(s_y, 1 + DT * j + t - 1)
                                after(t - 2)
                dve.wait_ge(s_y, 1 + DT * (j + 1))

            def add_to(where, i):
                part = where[:, bass.ds(i * (NB * D), NB * D)]
                return v.tensor_tensor(part, part, Y_ps, ALU.add)

            def add_bias(name):
                def f(where, i):
                    return v.tensor_tensor(where[:, bass.ds(i * (NB * D), NB * D)].rearrange("p (b d) -> p b d", d=D),
                                           Y_ps.rearrange("p (b d) -> p b d", d=D),
                                           vec[name][:, :].unsqueeze(1).to_broadcast([P, NB, D]), ALU.add)
                return f

            def scaled(where, i):
                return v.tensor_tensor(where[:, bass.ds(i * (NB * D), NB * D)].rearrange("p (b d) -> p b d", d=D),
                                       Y_ps.rearrange("p (b d) -> p b d", d=D),
                                       dinv[:, bass.ds(i * NB, NB)].unsqueeze(2).to_broadcast([P, NB, D]), ALU.mult)

            def copied(where, i):
                return v.tensor_copy(where[:, bass.ds(i * (NB * D), NB * D)], Y_ps)

            seeds = [0]

            def tile_pass(n):
                kind, o, heads, slope = PASSES[n]
                use = before(n, "max", "attend", "plain", "relate")
                att = before(n, "attend")
                where = {"max": (MX, H, heads), "plain": (acc, W, D)}.get(
                    kind, (acc, W, W if heads == H else D + 1))
                dloc = rec[o][:, :].bitcast(F32)
                links = 2 * {"max": PU, "plain": 0, "relate": 0, "attend": 3}[kind]

                def one_hot(i, ahead, g):
                    local = dloc[:, bass.ds((i * 2 + ahead) * (U * 4), U * 4)].rearrange("p (u f) -> p u f", f=4)[:, :, 1:2]
                    v.tensor_tensor((NE if kind == "max" else OH)[:, g * U:(g + 1) * U, :],
                                    iota_n[:, :].unsqueeze(1).to_broadcast([P, U, P]), local.to_broadcast([P, U, P]),
                                    ALU.not_equal if kind == "max" else ALU.is_equal).then_inc(s_oh, 1)

                def stage_targets(blocks, i, ahead, tiles=range(U)):
                    if ahead and tiles[0] == 0:
                        dve.wait_ge(s_edm, i * 2 + (att * (GROUPS + 1) + ahead))
                    for k in tiles:
                        ins = v.tensor_copy(target[:, k, :], EDB[:, bass.ds(blocks[k] * (3 * 2 * H), 3 * 2 * H)])
                    if tiles[-1] == U - 1:
                        ins.then_inc(s_target, 1)

                def edge_scores(i, ahead, g, meanwhile=()):
                    meanwhile = list(meanwhile) + [lambda: None] * 3
                    dve.wait_ge(s_edm, i * 2 + (att * (GROUPS + 1) + ahead + 1))
                    if ahead:
                        dve.wait_ge(s_den, i * 2 + (att * (GROUPS + 1) + ahead))
                    edm = EDM_ps.rearrange("p (u s h) -> p u s h", u=U, h=H)
                    s3 = SC[:, :].rearrange("p (u h) -> p u h", h=H)
                    order.mark(v.tensor_tensor(s3, ES[:, bass.ds((i * 2 + ahead) * (U * H), U * H)].rearrange("p (u h) -> p u h", h=H),
                                               edm[:, :, 0, :], ALU.add))
                    meanwhile[0]()
                    order.written()
                    order.mark(v.scalar_tensor_tensor(SC[:, :], SC[:, :], slope, SC[:, :], ALU.mult, ALU.max))
                    meanwhile[1]()
                    order.written()
                    order.mark(v.tensor_tensor(s3, s3, edm[:, :, 1, :], ALU.subtract))
                    meanwhile[2]()
                    order.written()
                    v.tensor_scalar(SC[:, :], SC[:, :], 0.0, None, ALU.min).then_inc(s_sc, 1)

                def message(i, g, q):
                    i, g = i + g // 2, g % 2
                    if kind == "attend" and q == 0:
                        dve.wait_ge(s_ex, i * 2 + (att * (GROUPS + 1) + g + 1))
                    s = slice(g * U + 2 * q, g * U + 2 * q + 2)
                    dve.wait_ge(landed[g * PU + q], i * 32 + 32 * (use * USES[g] + 1))
                    if kind == "relate":
                        dve.wait_ge(rel_landed[g * PU + q], i * 32 + 32)
                        ins = v.tensor_tensor(M[:, s, 0:D + 1], M[:, s, 0:D + 1], G[:, s, :], ALU.mult)
                    else:
                        weight = EX[:, g, :].rearrange("p (u h) -> p u h", h=H)[:, 2 * q:2 * q + 2, 0:heads]
                        c = D // heads
                        ins = v.tensor_tensor(M[:, s, 0:D].rearrange("p u (h c) -> p u h c", h=heads),
                                              G[:, s, 0:D].rearrange("p u (h c) -> p u h c", h=heads),
                                              weight.unsqueeze(3).to_broadcast([P, 2, heads, c]), ALU.mult)
                    ins.then_inc(s_msg, 1)

                def drain(i, g, k, blocks):
                    full, stride, w = where
                    part = full[:, bass.ds(blocks[k] * stride, w)]
                    if kind != "max":
                        dve.wait_ge(s_ps, i * (2 * U) + (n * T + g * U + k + 1))
                    dve.wait_ge(s_psfree, i * (2 * U) + (PRIME + n * T + g * U + k))
                    if kind == "max":
                        ins = v.tensor_tensor(part, part, edge_max[:, k, 0:heads], ALU.max)
                    else:
                        ins = v.tensor_tensor(part, part, ps[:, k % BANKS[kind], 0:w], ALU.add)
                    ins.then_inc(s_psfree, 1)

                def reduce(i, g, q):
                    dve.wait_ge(s_ps, i * (2 * U) + (n * T + g * U + 2 * q + 2))
                    dve.wait_ge(s_psfree, i * (2 * U) + (PRIME + n * T + g * U + max(2 * q - 2, 0)))
                    if q == PU - 1:
                        v.tensor_copy(ES[:, bass.ds((i * 2 + g) * (U * H), U * H)].rearrange("p (u h) -> p u h", h=H),
                                      G[:, g * U:(g + 1) * U, 0:H])
                    order.mark(v.tensor_reduce(edge_max[:, 2 * q:2 * q + 2, 0:heads],
                                               ps[:, 2 * q:2 * q + 2, 0:heads * P].rearrange("p t (h e) -> p t h e", h=heads),
                                               AX.X, ALU.max))

                def group(i, g, last=False):
                    if kind == "max":
                        reduce(i, g, 0)
                    if kind == "relate":
                        message(i, g, 0)
                    if kind in ("attend", "relate"):
                        message(i, g, 1)
                    one_hot(i, g + 1, 1 - g)
                    blocks = load_blocks(dve, o, (i * 2 + g) * U, 2 * U if kind == "attend" else U)
                    if kind == "attend":
                        stage_targets(blocks[U:], i, g + 1, range(U // 2))
                        drain(i, g, 0, blocks)
                        stage_targets(blocks[U:], i, g + 1, range(U // 2, U))
                        drain(i, g, 1, blocks)
                        message(i, g, 2)
                        drain(i, g, 2, blocks)
                        message(i, g, 3)
                        for k in (3, 4):
                            drain(i, g, k, blocks)
                        edge_scores(i, g + 1, 1 - g, [lambda: drain(i, g, 5, blocks)])
                        drain(i, g, 6, blocks)
                        if not last:
                            message(i, g + 1, 0)
                        drain(i, g, 7, blocks)
                    elif kind == "max":
                        for q in range(PU):
                            if q + 1 < PU:
                                reduce(i, g, q + 1)
                            order.written(but=int(q + 1 < PU))
                            drain(i, g, 2 * q, blocks)
                            drain(i, g, 2 * q + 1, blocks)
                    else:
                        for k in range(U):
                            drain(i, g, k, blocks)
                            if kind == "relate" and k in (1, 3):
                                message(i, g, k // 2 + 2)

                one_hot(0, 0, 0)
                if kind == "attend":
                    stage_targets(load_blocks(dve, o, 0, U), 0, 0)
                    edge_scores(0, 0, 0)
                if kind in ("plain", "attend"):
                    seeds[0] += 1
                    dve.wait_ge(s_seed, seeds[0])
                if kind == "attend":
                    message(0, 0, 0)
                with dve.Fori(0, LOOP) as i:
                    order.enter(i, links)
                    group(i, 0)
                    group(i, 1)
                    order.leave(LOOP)
                group(LOOP, 0, last=True)
                L(v.memset(st1[:, :], 0.0))

            roots, norms = [0], [0]

            def inverse_root(dest):
                roots[0] += 1
                dve.wait_ge(s_sq, roots[0])
                L(v.reciprocal(dest[:, :], st2[:, :]))

            def blocks_of(a3, t):
                return a3[:, t * NB:(t + 1) * NB, :]

            def turn_of(st, t):
                return st[:, t * NB:(t + 1) * NB].unsqueeze(2).to_broadcast([P, NB, D])

            def row_of(name):
                return vec[name][:, :].unsqueeze(1).to_broadcast([P, NB, D])

            def normed(a3, gamma=None, beta=None):
                def feed(t):
                    a = blocks_of(a3, t)
                    ins = v.tensor_tensor(a, a, turn_of(st2, t), ALU.mult)
                    if gamma is not None:
                        L(ins)
                        L(v.tensor_tensor(a, a, row_of(gamma), ALU.mult))
                        ins = v.tensor_tensor(a, a, row_of(beta), ALU.add)
                    ins.then_inc(s_in, 1)
                return feed

            def layer_norm(a3):
                L(v.tensor_reduce(st1[:, :], a3, AX.X, ALU.add))
                L(v.tensor_scalar(st1[:, :], st1[:, :], 1.0 / D, None, ALU.mult))
                for t in range(DT):
                    a = blocks_of(a3, t)
                    v.tensor_tensor(a, a, turn_of(st1, t), ALU.subtract).then_inc(s_centred, 1)
                for t in range(DT):
                    norms[0] += 1
                    dve.wait_ge(s_squared, norms[0])
                    order.mark(v.tensor_reduce(st2[:, t * NB:(t + 1) * NB], blocks_of(tmp3, t), AX.X, ALU.add))
                order.written()
                v.tensor_scalar(st2[:, :], st2[:, :], 1.0 / D, LN_EPS, ALU.mult, ALU.add).then_inc(s_sq_in, 1)
                inverse_root(st2)

            EDM4 = EDM[:, :].rearrange("p (b s h) -> p b s h", s=2, h=H)
            ESN3 = ESN[:, :].rearrange("p (b h) -> p b h", h=H)
            MX3 = MX[:, :].rearrange("p (b h) -> p b h", h=H)
            exs3 = exs[:, :].rearrange("p (b h) -> p b h", h=H)

            def score(dest, a, heads, at=slice(0, B)):
                L(v.tensor_tensor(H3[:, at, :], Y3[:, at, :],
                                  vec[a][:, :].unsqueeze(1).to_broadcast([P, at.stop - at.start, D]), ALU.mult))
                L(v.tensor_reduce(dest[:, at, 0:heads], H3[:, at, :].rearrange("p b (h c) -> p b h c", h=heads), AX.X, ALU.add))

            def source_scores(a, heads):
                return lambda t: score(ESN3, a, heads, slice(t * NB, (t + 1) * NB))

            def maxima(slope):
                m = EDM4[:, :, 1, :]
                L(v.tensor_tensor(m, MX3, EDM4[:, :, 0, :], ALU.add))
                L(v.scalar_tensor_tensor(m, m, slope, m, ALU.mult, ALU.max))

            def split_targets():
                parts = EDB[:, :].rearrange("p (b s h) -> p b s h", s=3, h=2 * H)
                rest = left[:, :].rearrange("p (b h) -> p b h", h=2 * H)
                L(v.tensor_copy(left[:, :], EDM[:, :]))
                for part in range(3):
                    L(v.tensor_copy(parts[:, :, part, :], rest))
                    if part < 2:
                        L(v.tensor_tensor(rest, rest, parts[:, :, part, :], ALU.subtract))

            nul_b = exs[:, 0:B]
            dve.wait_ge(s_const, 2)
            v.memset(exs[:, :], 0.0)
            v.memset(zero[:, :], 0.0)
            v.memset(ESN[:, :], 0.0)
            v.memset(EDM[:, :], 0.0)
            v.memset(edge_max[:, :, :], 0.0)
            v.memset(deg["src"][:, :], 0.0)
            v.memset(deg["dst"][:, :], 0.0)
            v.tensor_copy(iota_n[:, :], iota_i[:, 0:P])
            v.tensor_copy(iota_t, iota_i[:, 0:T])
            v.memset(ES[:, T * H:TX * H], 0.0)
            for o in ("src", "dst"):
                v.memset(rec[o][:, T * 4:TX * 4].bitcast(F32), -1.0)
                v.memset(block_of[o][:, T:T + U], 0)
            L(v.memset(fill, 0.0))
            v.memset(fill.rearrange("p (t f) -> p t f", f=4)[:, :, 1:2], -1.0).then_inc(s_fill, 1)
            dve.sem_inc(s_psfree, PRIME)
            for s in (s_y, s_y_ps, s_xt_ps, s_hist):
                dve.sem_inc(s, 1)
            dve.wait_ge(s_load, 16 * 3)
            L(v.tensor_copy(ident_b[:, :], ident[:, :]))
            for h in range(H):
                L(v.tensor_scalar(neg_ident[:, h, :], ident[:, :], -BIG, None, ALU.mult))
            dve.wait_ge(s_filled, 32)
            for n, o in enumerate(("src", "dst")):
                sort(n, o)
                degrees(n, o)
            def attention(n_max, n_att, heads, slope, dst_vec, self_loop):
                if not self_loop:
                    L(v.tensor_scalar(ESN3[:, :, 0:1], ESN3[:, :, 0:1], sc[:, 1:2], None, ALU.add))
                v.tensor_copy(exs[:, :], ESN[:, :]).then_inc(s_tab_sc, 1)
                score(EDM4[:, :, 0, :], dst_vec, heads)
                if not self_loop:
                    L(v.tensor_scalar(EDM4[:, :, 0, 0:1], EDM4[:, :, 0, 0:1], sc[:, 0:1], None, ALU.add))
                    dve.wait_ge(s_rec["src"], 16)
                    dve.wait_ge(s_rec["dst"], 16)
                dve.sem_inc(s_acc, 1)
                if self_loop:
                    L(v.tensor_copy(MX[:, :], ESN[:, :]))
                else:
                    L(v.memset(MX[:, :], -BIG))
                tile_pass(n_max)
                maxima(slope)
                split_targets()
                tile_pass(n_att)
                if self_loop:
                    L(v.tensor_tensor(exs3, ESN3, EDM4[:, :, 0, :], ALU.add))
                    L(v.scalar_tensor_tensor(exs[:, :], exs[:, :], slope, exs[:, :], ALU.mult, ALU.max))
                    v.tensor_tensor(exs3, exs3, EDM4[:, :, 1, :], ALU.subtract).then_inc(s_self, 1)

            def attended_rectified(t):
                h = blocks_of(H3, t)
                L(v.tensor_tensor(h, blocks_of(tmp3, t), row_of("b1"), ALU.add))
                v.scalar_tensor_tensor(h, h, 0.0, blocks_of(X3, t), ALU.max, ALU.add).then_inc(s_in, 1)

            def attended(t):
                v.tensor_tensor(blocks_of(H3, t), blocks_of(tmp3, t), row_of("b2"), ALU.add).then_inc(s_in, 1)

            n_self = 0
            for step in PLAN:
                what = step[0]
                if what == "degrees":
                    v.tensor_scalar(st2[:, :], deg["dst"][:, :], 1.0, None, ALU.add).then_inc(s_sq_in, 1)
                    inverse_root(dinv)
                elif what == "L0":
                    dve.wait_ge(s_loadx, 16 * RAW_LOADS)
                    for s_, turns in zip(s_sorted, STAGE_TURNS):
                        dve.wait_ge(s_, 16 * SC_U * turns)
                    dve.sem_inc(s_in, DT)
                    product(0, add_bias("b_layer"), after=source_scores("w_a2", 1))
                    dve.sem_inc(s_tab, 1)
                    attention(0, 1, 1, SLOPE0, "w_a1", False)
                    den = acc3[:, :, D:D + 1]
                    L(v.tensor_scalar(den, den, 1e-30, None, ALU.max))
                    L(v.reciprocal(st1[:, :].unsqueeze(2), den))
                    L(v.tensor_tensor(tmp3, tmp3, nb(st1[:, :]), ALU.mult))
                    L(v.tensor_tensor(X3, X3, tmp3, ALU.add))
                    layer_norm(X3)
                elif what == "L1in":
                    product(1, add_bias("b_in"), normed(X3))
                elif what == "conv":
                    l = step[1]
                    if l == 0:
                        dve.sem_inc(s_in, DT)
                    product(2 + l, scaled, normed(H3, "gamma", "beta") if l else None)
                    dve.sem_inc(s_tab, 1)
                    bias = vb(vec[f"bs{l}"][:, :])
                    if l == 0:
                        L(v.tensor_tensor(H3, H3, bias, ALU.add))
                        L(v.tensor_tensor(X3, X3, vb(vec["b_out"][:, :]), ALU.add))
                    else:
                        L(v.tensor_scalar(Hh, Hh, 0.0, None, ALU.max))
                        L(v.tensor_tensor(H3, H3, bias, ALU.add))
                    tile_pass(2 + l)
                    L(v.tensor_tensor(tmp3, tmp3, nb(dinv[:, :]), ALU.mult))
                    L(v.tensor_tensor(H3, H3, tmp3, ALU.add))
                    layer_norm(H3)
                elif what == "L1out":
                    product(5, add_to, normed(H3, "gamma", "beta"))
                    layer_norm(X3)
                elif what == "gat":
                    l = step[1]
                    sfx = ("1", "2", "n")[l]
                    product(6 + l, copied, (normed(X3), attended_rectified, attended)[l], source_scores("as" + sfx, H))
                    dve.sem_inc(s_tab, 1)
                    attention(5 + 2 * l, 6 + 2 * l, H, SLOPE2, "ad" + sfx, True)
                elif what == "self":
                    l = step[1]
                    n_self += 1
                    dve.wait_ge(s_selfx, n_self)
                    den = acc3[:, :, D:W]
                    L(v.tensor_tensor(den, den, exs3, ALU.add))
                    L(v.tensor_scalar(den, den, GAT_EPS, None, ALU.add))
                    c = D // H
                    for h in range(H):
                        yh, ah = Y3[:, :, h * c:(h + 1) * c], acc3[:, :, h * c:(h + 1) * c]
                        L(v.tensor_tensor(yh, yh, exs3[:, :, h:h + 1].to_broadcast([P, B, c]), ALU.mult))
                        L(v.tensor_tensor(ah, ah, yh, ALU.add))
                    L(v.reciprocal(exs3, den))
                    for h in range(H):
                        ah = acc3[:, :, h * c:(h + 1) * c]
                        L(v.tensor_tensor(ah, ah, exs3[:, :, h:h + 1].to_broadcast([P, B, c]), ALU.mult))
                    if l == 2:
                        L(v.tensor_tensor(H3, tmp3, vb(vec["bn"][:, :]), ALU.add))
                        L(v.tensor_tensor(Hh, Hh, X[:, :], ALU.add))
                        L(v.scalar_tensor_tensor(X[:, :], Hh, 0.0, X[:, :], ALU.max, ALU.add))
                        layer_norm(X3)
                        L(v.tensor_tensor(X3, X3, nb(st2[:, :]), ALU.mult))
                elif what == "gate":
                    dve.sem_inc(s_hfree, 1)
                    dve.wait_ge(s_relld, 16)
                    gr = R4[:, :, 0:D].rearrange("p q (k c) -> p q k c", k=4)
                    gwr = gw[0:EP, :].rearrange("p (c k) -> p k c", k=4)
                    for q in range(4):
                        L(v.tensor_tensor(R4t[:, q, :].rearrange("p (k c) -> p k c", k=4), gr[:, q, :, :], gwr, ALU.mult))
                    L(v.tensor_reduce(cnt[0:EP, 0:4], R4t, AX.X, ALU.add))
                    v.tensor_scalar(cnt[0:EP, 0:4], cnt[0:EP, 0:4], sc[0:EP, 2:3], None, ALU.add).then_inc(s_gz, 1)
                    dve.wait_ge(s_gs, 1)
                    L(v.tensor_scalar(cnt[0:EP, 0:4], cnt[0:EP, 0:4], 1.0, None, ALU.add))
                    L(v.reciprocal(cnt[0:EP, 0:4], cnt[0:EP, 0:4]))
                    L(v.tensor_tensor(R4[:, :, 0:D], R4[:, :, 0:D],
                                      cnt[0:EP, 0:4].unsqueeze(2).to_broadcast([EP, 4, D]), ALU.mult))
                    v.tensor_copy(R4[:, :, D:D + 1], cnt[0:EP, 0:4].unsqueeze(2)).then_inc(s_rel, 1)
                elif what == "relate":
                    v.tensor_scalar(st2[:, :], deg["src"][:, :], 1.0, None, ALU.max).then_inc(s_sq_in, 1)
                    inverse_root(dinv)
                    L(v.tensor_tensor(scaled3[:, :, 0:D], X3, nb(dinv[:, :]), ALU.mult))
                    v.tensor_copy(scaled3[:, :, D:D + 1], dinv[:, :].unsqueeze(2)).then_inc(s_tab, 1)
                    dve.wait_ge(s_tab_st, 16 * 8)
                    L(v.memset(acc[:, :], 0.0))
                    tile_pass(11)
                    dve.wait_ge(s_relst, 16)
                    v.tensor_scalar(st2[:, :], deg["dst"][:, :], 1.0, None, ALU.max).then_inc(s_sq_in, 1)
                    inverse_root(dinv)
                    L(v.tensor_tensor(st2[:, :].unsqueeze(2), acc3[:, :, D:D + 1], dinv[:, :].unsqueeze(2), ALU.mult))

                    def messages(t):
                        v.tensor_tensor(blocks_of(H3, t), blocks_of(tmp3, t), turn_of(dinv, t), ALU.mult).then_inc(s_in, 1)
                        dve.wait_ge(s_in, DT * 9 + t + 1)
                        L(v.tensor_tensor(blocks_of(tmp3, t), row_of("msg_b"), turn_of(st2, t), ALU.mult))

                    def updated(t):
                        h = blocks_of(H3, t)
                        L(v.tensor_tensor(h, blocks_of(X3, t), blocks_of(Y3, t), ALU.add))
                        v.tensor_tensor(h, h, blocks_of(tmp3, t), ALU.add).then_inc(s_in, 1)

                    product(9, copied, messages)
                    product(10, add_bias("upd_b"), updated)
                    for k in range(4):
                        xk = X[:, :].rearrange("p (n k) -> p n k", k=4)[:, :, k:k + 1].rearrange("p (b c) k -> p b (c k)", c=D // 4)
                        L(v.tensor_tensor(xk, xk, Y3[:, :, k * (D // 4):(k + 1) * (D // 4)], ALU.add))
                    layer_norm(X3)
                    L(v.tensor_tensor(X3, X3, nb(st2[:, :]), ALU.mult))
                    dve.sem_inc(s_out, 1)


PLAN = [("degrees",), ("root",),
        ("L0",), ("product", 0), ("zero",), ("pass", 0), ("pass", 1), ("square", "X"), ("root",),
        ("L1in",), ("product", 1),
        ("conv", 0), ("product", 2), ("pass", 2), ("square", "H"), ("root",),
        ("conv", 1), ("product", 3), ("pass", 3), ("square", "H"), ("root",),
        ("conv", 2), ("product", 4), ("pass", 4), ("square", "H"), ("root",),
        ("L1out",), ("product", 5), ("square", "X"), ("root",),
        ("gat", 0), ("product", 6), ("zero",), ("pass", 5), ("pass", 6), ("self", 0),
        ("gat", 1), ("product", 7), ("zero",), ("pass", 7), ("pass", 8), ("self", 1),
        ("gat", 2), ("product", 8), ("zero",), ("pass", 9), ("pass", 10), ("self", 2), ("square", "X"), ("root",),
        ("gate",), ("relate",), ("root",), ("pass", 11), ("root",), ("product", 9), ("product", 10),
        ("square", "X"), ("root",)]

_NAMES = ["x", "src", "dst", "edge_type_500", "L0_gnn_W_layer", "L0_gnn_b_layer", "L0_gnn_w_a1", "L0_gnn_b_a1",
          "L0_gnn_w_a2", "L0_gnn_b_a2", "L1_gnn_W_in", "L1_gnn_b_in", "L1_gnn_Ws", "L1_gnn_bs", "L1_gnn_gamma",
          "L1_gnn_beta", "L1_gnn_W_out", "L1_gnn_b_out", "L2_gnn_W1", "L2_gnn_as1", "L2_gnn_ad1", "L2_gnn_b1",
          "L2_gnn_W2", "L2_gnn_as2", "L2_gnn_ad2", "L2_gnn_b2", "L2_gnn_WN", "L2_gnn_asN", "L2_gnn_adN", "L2_gnn_bN",
          "L3_gnn_relation_emb", "L3_gnn_msg_w", "L3_gnn_msg_b", "L3_gnn_upd_w", "L3_gnn_upd_b", "L3_gnn_gate_w",
          "L3_gnn_gate_b"]


def kernel(**inputs):
    import concourse.bacc as bacc
    from concourse.bass_utils import run_bass_kernel_spmd

    nc = bacc.Bacc("TRN2", target_bir_lowering=False, num_devices=1)
    arrays, a = {}, {}
    for name in _NAMES:
        v = np.ascontiguousarray(inputs[name])
        arrays["in_" + name] = v
        a[name] = nc.dram_tensor("in_" + name, v.shape, mybir.dt.from_np(v.dtype), kind="ExternalInput").ap()
    out = nc.dram_tensor("out", (N, D), F32, kind="ExternalOutput").ap()
    row = lambda ap: ap.rearrange("a b -> (a b)")
    mats = {"w_layer": a["L0_gnn_W_layer"], "w_in": a["L1_gnn_W_in"], "ws0": a["L1_gnn_Ws"][0], "ws1": a["L1_gnn_Ws"][1],
            "ws2": a["L1_gnn_Ws"][2], "w_out": a["L1_gnn_W_out"], "w1": a["L2_gnn_W1"], "w2": a["L2_gnn_W2"],
            "wn": a["L2_gnn_WN"]}
    vecs = {"b_layer": a["L0_gnn_b_layer"], "w_a1": row(a["L0_gnn_w_a1"]), "w_a2": row(a["L0_gnn_w_a2"]),
            "b_in": a["L1_gnn_b_in"], "bs0": a["L1_gnn_bs"][0], "bs1": a["L1_gnn_bs"][1], "bs2": a["L1_gnn_bs"][2],
            "gamma": a["L1_gnn_gamma"], "beta": a["L1_gnn_beta"], "b_out": a["L1_gnn_b_out"],
            "as1": row(a["L2_gnn_as1"]), "ad1": row(a["L2_gnn_ad1"]), "b1": a["L2_gnn_b1"],
            "as2": row(a["L2_gnn_as2"]), "ad2": row(a["L2_gnn_ad2"]), "b2": a["L2_gnn_b2"],
            "asn": row(a["L2_gnn_asN"]), "adn": row(a["L2_gnn_adN"]), "bn": a["L2_gnn_bN"],
            "msg_b": row(a["L3_gnn_msg_b"]), "upd_b": row(a["L3_gnn_upd_b"])}
    gnn_program(nc, a["x"], a["src"], a["dst"], a["edge_type_500"], mats, vecs,
                [a["L0_gnn_b_a1"], a["L0_gnn_b_a2"], a["L3_gnn_gate_b"]], a["L3_gnn_relation_emb"],
                row(a["L3_gnn_gate_w"]), {"msg": a["L3_gnn_msg_w"], "upd": a["L3_gnn_upd_w"]}, out)
    r = run_bass_kernel_spmd(nc, [arrays], core_ids=[0])
    return r.results[0]["out"]
```
